# Optimizing a Trainium2 kernel written in Bass

```python
import numpy as np
import jax
import jax.numpy as jnp

def _softmax(x, axis=-1):
    return jax.nn.softmax(x, axis=axis)

def _gelu(x):
    return jax.nn.gelu(x, approximate=True)

def _silu(x):
    return jax.nn.silu(x)

def _sigmoid(x):
    return jax.nn.sigmoid(x)

def _layernorm(x, axis=-1, eps=1e-05):
    m = jnp.mean(x, axis=axis, keepdims=True)
    v = jnp.var(x, axis=axis, keepdims=True)
    return (x - m) / jnp.sqrt(v + eps)

def _scatter_add(tgt, idx, src, axis=0):
    return tgt.at[idx].add(src)

def _segment_sum(src, seg, n):
    return jax.ops.segment_sum(src, seg, n)
kernel_name = 'mk_metaformer_d1_conv_nchw256_r4_a75ec5'

def setup_inputs(seed: int=0):
    np.random.seed(seed)
    _w = jnp.asarray

    def _rec_inputs():
        import jax
        import jax.numpy as jnp
        _gk = jax.random.key(seed)
        x = 7.22e-05 + 1 * jax.random.normal(jax.random.fold_in(_gk, 1), (8, 64, 16, 16), jnp.float32)
        return x
    x = _rec_inputs()

    def _L0_conv_setup():
        import jax, jax.numpy as jnp
        import numpy as np
        key = jax.random.key(seed)
        ks = jax.random.split(key, 7)
        B, C, H, W = (8, 64, 16, 16)
        Ck, Cv, Co = (32, 32, 64)
        s = lambda fan_in: 1.0 / np.sqrt(fan_in)
        return {'x': jax.random.normal(ks[0], (B, C, H, W), dtype=jnp.float32), 'w_kq': jax.random.normal(ks[1], (Ck, C), dtype=jnp.float32) * s(C), 'b_kq': jax.random.normal(ks[2], (Ck,), dtype=jnp.float32) * s(C), 'w_v': jax.random.normal(ks[3], (Cv, C), dtype=jnp.float32) * s(C), 'b_v': jax.random.normal(ks[4], (Cv,), dtype=jnp.float32) * s(C), 'w_o': jax.random.normal(ks[5], (Co, Cv), dtype=jnp.float32) * s(Cv), 'b_o': jax.random.normal(ks[6], (Co,), dtype=jnp.float32) * s(Cv)}
    _L0_conv_all = _L0_conv_setup()
    _L0_conv_in = {k: v for k, v in _L0_conv_all.items() if k in ('w_kq', 'b_kq', 'w_v', 'b_v', 'w_o', 'b_o')}
    del _L0_conv_all

    def _L0_ffn_setup():
        import jax, jax.numpy as jnp
        import numpy as np
        N_EXPERTS = 8
        TOP_K = 2
        key = jax.random.key(seed)
        ks = jax.random.split(key, 5)
        B, T, C, E, H = (8, 512, 64, 8, 682)
        scale = 1.0 / np.sqrt(C)
        return {'x': jax.random.normal(ks[0], (B, T, C), dtype=jnp.float32), 'router_w': jax.random.normal(ks[1], (E, C), dtype=jnp.float32) * scale, 'w1': jax.random.normal(ks[2], (E, H, C), dtype=jnp.float32) * scale, 'w2': jax.random.normal(ks[3], (E, C, H), dtype=jnp.float32) * (1.0 / np.sqrt(H)), 'w3': jax.random.normal(ks[4], (E, H, C), dtype=jnp.float32) * scale}
    _L0_ffn_all = _L0_ffn_setup()
    _L0_ffn_in = {k: v for k, v in _L0_ffn_all.items() if k in ('router_w', 'w1', 'w2', 'w3')}
    del _L0_ffn_all
    return {'x': x, 'L0_conv_w_kq': _L0_conv_in['w_kq'], 'L0_conv_b_kq': _L0_conv_in['b_kq'], 'L0_conv_w_v': _L0_conv_in['w_v'], 'L0_conv_b_v': _L0_conv_in['b_v'], 'L0_conv_w_o': _L0_conv_in['w_o'], 'L0_conv_b_o': _L0_conv_in['b_o'], 'L0_ffn_router_w': _L0_ffn_in['router_w'], 'L0_ffn_w1': _L0_ffn_in['w1'], 'L0_ffn_w2': _L0_ffn_in['w2'], 'L0_ffn_w3': _L0_ffn_in['w3']}

def reference(x, L0_conv_w_kq, L0_conv_b_kq, L0_conv_w_v, L0_conv_b_v, L0_conv_w_o, L0_conv_b_o, L0_ffn_router_w, L0_ffn_w1, L0_ffn_w2, L0_ffn_w3):
    import jax
    import jax.numpy as jnp

    def _L0_conv_ref(x, w_kq, b_kq, w_v, b_v, w_o, b_o):
        import jax, jax.numpy as jnp
        import numpy as np
        B, C, H, W = x.shape
        N = H * W
        xf = x.reshape(B, C, N)
        kq = jnp.einsum('kc,bcn->bkn', w_kq, xf) + b_kq[None, :, None]
        v = jnp.einsum('vc,bcn->bvn', w_v, xf) + b_v[None, :, None]
        sim = jnp.einsum('bkn,bkm->bnm', kq, kq)
        attn = jax.nn.softmax(sim, axis=-1)
        ctx = jnp.einsum('bnm,bvm->bvn', attn, v)
        out = jnp.einsum('ov,bvn->bon', w_o, ctx) + b_o[None, :, None]
        return out.reshape(B, -1, H, W)

    def _L0_ffn_ref(x, router_w, w1, w2, w3):
        import jax, jax.numpy as jnp
        import numpy as np
        N_EXPERTS = 8
        TOP_K = 2
        B, T, C = x.shape
        flat = x.reshape(-1, C)
        logits = flat @ router_w.T
        probs = jax.nn.softmax(logits, axis=-1)
        topk_probs, topk_idx = jax.lax.top_k(probs, TOP_K)
        topk_probs = topk_probs / (jnp.sum(topk_probs, axis=-1, keepdims=True) + 1e-09)
        onehot = jax.nn.one_hot(topk_idx, N_EXPERTS, dtype=flat.dtype)
        gates = jnp.einsum('nk,nke->ne', topk_probs, onehot)
        h1 = jnp.einsum('nc,ehc->neh', flat, w1)
        h3 = jnp.einsum('nc,ehc->neh', flat, w3)
        h = jax.nn.silu(h1) * h3
        y = jnp.einsum('neh,ech->nec', h, w2)
        out = jnp.einsum('ne,nec->nc', gates, y)
        return out.reshape(B, T, C)

    def _gn(v, G=32, eps=1e-05):
        B_, C_, H_, W_ = v.shape
        g = v.reshape(B_, G, C_ // G, H_, W_)
        m = jnp.mean(g, axis=(2, 3, 4), keepdims=True)
        s = jnp.var(g, axis=(2, 3, 4), keepdims=True)
        return ((g - m) / jnp.sqrt(s + eps)).reshape(v.shape)

    def _ln_c(v, eps=1e-06):
        m = jnp.mean(v, axis=1, keepdims=True)
        s = jnp.var(v, axis=1, keepdims=True)
        return (v - m) / jnp.sqrt(s + eps)

    def _ln_t(v, eps=1e-05):
        m = jnp.mean(v, axis=-1, keepdims=True)
        s = jnp.var(v, axis=-1, keepdims=True)
        return (v - m) / jnp.sqrt(s + eps)

    def _to_tokens(v):
        B_, C_, H_, W_ = v.shape
        return v.reshape(B_, C_, H_ * W_).transpose(0, 2, 1)

    def _from_tokens(t, like):
        B_, C_, H_, W_ = like.shape
        return t.transpose(0, 2, 1).reshape(B_, C_, H_, W_)
    x = x + _L0_conv_ref(_ln_c(x), L0_conv_w_kq, L0_conv_b_kq, L0_conv_w_v, L0_conv_b_v, L0_conv_w_o, L0_conv_b_o)
    t = _to_tokens(x)
    t = t + _L0_ffn_ref(_ln_t(t), L0_ffn_router_w, L0_ffn_w1, L0_ffn_w2, L0_ffn_w3)
    x = _from_tokens(t, x)
    return x

_drawn_inputs = setup_inputs


def setup_inputs(seed=0):
    import zlib

    import numpy as np

    out = dict(_drawn_inputs(seed))
    spreads = {}
    factors = {'L0_conv_b_kq': 4.796}
    for name, (base, spread) in spreads.items():
        noise = np.random.default_rng([zlib.crc32(name.encode()), seed]).standard_normal(out[name].shape)
        drawn = base * np.exp(spread * noise) if base else spread * noise
        out[name] = jnp.asarray(drawn.astype(out[name].dtype))
    for name, factor in factors.items():
        out[name] = (out[name] * factor).astype(out[name].dtype)
    return out
```

```python
from contextlib import ExitStack

import concourse.bass as bass
from concourse import mybir

F32 = mybir.dt.float32
F32R = mybir.dt.float32r
ALU = mybir.AluOpType
ACT = mybir.ActivationFunctionType
AX = mybir.AxisListType

B, C, N = 8, 64, 256
CK = 32
E, H = 8, 682
P = 128
TILES = B * N // P
BLK = 512
NBLK = B * N // BLK
TPB = BLK // P
BPB = BLK // N
PAIRS = E // 2
CHUNKS = -(-2 * H // P)
SEAM = H // P
SLOTS = SEAM + 1
PW = CHUNKS * P
STEPS = PAIRS * CHUNKS
LAG = 4
RING = 4
ROT = 16
DVE_LO = [s for s in range(STEPS) if s % 4 == 3]


def metaformer(nc, x_tok, wk_aug, wv_aug, wo_t, b_o, router_t, w1_t, w3_t, w2_t, out):
    with ExitStack() as ctx:
        def sb(name, shape, dt=F32):
            return ctx.enter_context(nc.sbuf_tensor(name, shape, dt))

        def sem(name):
            return ctx.enter_context(nc.semaphore(name))

        bank = [ctx.enter_context(nc.psum_tensor(f"bank{i}", [P, BLK], F32)) for i in range(8)]

        ident = sb("ident", [P, P])
        earlier = sb("earlier", [P, E, E])
        neg_half = sb("neg_half", [P, TPB])
        last_row = sb("last_row", [1, C + 1])
        pick_gate = sb("pick_gate", [2 * E, E, P], F32R)
        fold = sb("fold", [P, C])
        w1_raw = sb("w1_raw", [P, 2, PW])
        w3_raw = sb("w3_raw", [P, 2, PW])
        w2_raw = sb("w2_raw", [P, 2, 2 * SLOTS, C])
        w1_split = sb("w1_split", [P, PAIRS, PW], F32R)
        w3_split = sb("w3_split", [P, PAIRS, PW], F32R)
        w2_split = sb("w2_split", [P, PAIRS * 2 * SLOTS, 2, C], F32R)
        wk = sb("wk", [C + 1, CK])
        wv = sb("wv", [CK, C + 1])
        wo = sb("wo", [CK, C])
        bo = sb("bo", [1, C])
        wu = sb("wu", [C + 1, C + 1])
        router_raw = sb("router_raw", [P, E])
        router = sb("router", [P, E], F32R)
        x_sb = sb("x_sb", [P, TILES, C])
        xn = sb("xn", [P, TILES, C])
        t_sb = sb("t_sb", [P, TILES, C])
        tn = sb("tn", [P, 2, TPB, 2, C])
        cent = sb("cent", [P, TPB, C])
        sq = sb("sq", [P, TPB, C])
        mean = sb("mean", [P, TPB])
        ssq = sb("ssq", [P, TPB])
        var = sb("var", [P, 2, TILES])
        rstd = sb("rstd", [P, 2, TILES])
        xT = sb("xT", [C + 1, 2, BLK])
        kq = sb("kq", [CK, 2, BLK])
        t_hi = sb("t_hi", [P, NBLK * BLK], F32R)
        t_lo = sb("t_lo", [P, NBLK * BLK], F32R)
        tT = sb("tT", [C, NBLK * BLK])
        u_sb = sb("u_sb", [P, TILES, C + 1])
        neg_max = sb("neg_max", [P, B, 2])
        probs = sb("probs", [P, 2, 2, N])
        probsT = sb("probsT", [P, 2, 2, N])
        inv_sum = sb("inv_sum", [P, B, 2])
        logits = sb("logits", [P, TILES, E])
        small = sb("small", [P, 5, TILES])
        expo = sb("expo", [P, TILES, E])
        picked = sb("picked", [P, TILES, E])
        gates = sb("gates", [P, TILES, 2, E], F32R)
        gate_stage = sb("gate_stage", [P, TPB, 2 * E])
        gateT = sb("gateT", [2 * E, BLK], F32R)
        act_sb = sb("act_sb", [P, 2, BLK])
        hid = sb("hid", [P, RING, BLK])
        hid_hi = sb("hid_hi", [P, RING, BLK], F32R)
        hid_lo = sb("hid_lo", [P, RING, BLK], F32R)
        gate_b = sb("gate_b", [P, 2, BLK])
        gated = sb("gated", [P, BLK])
        acc = sb("acc", [P, BLK])
        cmp_gt = hid[:, 0:2, :].rearrange("p a (t e f) -> p (a t) e f", e=E, f=E)
        cmp_eq = hid[:, 2:4, :].rearrange("p a (t e f) -> p (a t) e f", e=E, f=E)

        x_loaded = [sem(f"x_loaded{k}") for k in range(NBLK)]
        consts_loaded = sem("consts_loaded")
        raw_loaded = [sem("raw_loaded0"), sem("raw_loaded1")]
        stored = sem("stored")
        consts_made = sem("consts_made")
        pool_step = sem("pool_step")
        dve_step = sem("dve_step")
        dve_consts = sem("dve_consts")
        var_ready = sem("var_ready")
        rstd_ready = sem("rstd_ready")
        xn_ready = sem("xn_ready")
        xT_done, xT_copied = sem("xT_done"), sem("xT_copied")
        kq_done, kq_copied = sem("kq_done"), sem("kq_copied")
        u_done, u_copied = sem("u_done"), sem("u_copied")
        wu_done, wu_copied = sem("wu_done"), sem("wu_copied")
        sim_done = sem("sim_done")
        max_ready = sem("max_ready")
        probs_ready = sem("probs_ready")
        probsT_done = sem("probsT_done")
        probsT_copied = [sem("probsT_copied_dve"), sem("probsT_copied_act")]
        attn_done = sem("attn_done")
        sum_inverted = sem("sum_inverted")
        t_ready = sem("t_ready")
        tn_ready = sem("tn_ready")
        tnT_done = sem("tnT_done")
        hi_ready, lo_ready = sem("t_hi_ready"), sem("t_lo_ready")
        tT_done, tT_copied = sem("tT_done"), sem("tT_copied")
        logits_done, logits_copied = sem("logits_done"), sem("logits_copied")
        shifted, exponents = sem("shifted"), sem("exponents")
        gates_ready = sem("gates_ready")
        w_hi_made, w_lo_made = sem("w_hi_made"), sem("w_lo_made")
        h1_done, h3_done = sem("h1_done"), sem("h3_done")
        silu_done = sem("silu_done")
        hid_done = sem("hid_done")
        hid_hi_made = sem("hid_hi_made")
        hid_lo_pool, hid_lo_dve = sem("hid_lo_pool"), sem("hid_lo_dve")
        hid_used = sem("hid_used")
        stage_copied = sem("stage_copied")
        gateT_done = sem("gateT_done")
        bank6_read = sem("bank6_read")
        spread_done, spread_copied = sem("spread_done"), sem("spread_copied")
        y_gated = sem("y_gated")
        acc_added = sem("acc_added")
        fold_done = sem("fold_done")

        S_BANK, PT_BANK, O_BANK = bank[0:2], bank[2:4], bank[4:6]
        H1_BANK, H3_BANK, Y_BANK = bank[0:2], bank[2:4], bank[4:6]
        CONST_DMAS = 6
        RAW_DMAS = 5

        def tiles(k):
            return slice(TPB * k, TPB * (k + 1))

        def cols(k):
            return slice(BLK * k, BLK * (k + 1))

        def step_no(base, place):
            return base * STEPS + place

        def lo_wait(eng, base, place):
            blk, s = divmod(place, STEPS)
            n_dve = sum(d < s for d in DVE_LO)
            if s in DVE_LO:
                eng.wait_ge(hid_lo_dve, base * len(DVE_LO) + blk * len(DVE_LO) + n_dve + 1)
            else:
                n_pool = STEPS - len(DVE_LO)
                eng.wait_ge(hid_lo_pool, base * n_pool + blk * n_pool + s - n_dve + 1)

        FIRST = [CHUNKS * (e // 2) + SEAM * (e % 2) for e in range(E)]
        LAST = [f + SEAM for f in FIRST]
        SPREAD_AT = {f + LAG: e for e, f in enumerate(FIRST)}
        SPREAD_COPY_AT = {f + LAG + 1: e for e, f in enumerate(FIRST)}
        GATE_AT = {(l + LAG + 1) % STEPS: (e, (l + LAG + 1) // STEPS) for e, l in enumerate(LAST)}
        FOLD_AT, RESULT_AT = LAG + 2, LAG + 3
        TAIL = LAG + 4

        def run_blocks(eng, tick):
            for place in range(ROT):
                tick(0, place, first=True, tail=False)
            with eng.Fori(0, NBLK - 1) as blk:
                for place in range(ROT, STEPS + ROT):
                    tick(blk, place, first=False, tail=False)
            for place in range(ROT, STEPS + TAIL):
                tick(NBLK - 1, place, first=False, tail=place >= STEPS)

        block = ctx.enter_context(nc.Block())

        @block.sync
        def _(sp):
            for k in range(NBLK):
                sp.dma_start(x_sb[:, tiles(k), :], x_tok[:, tiles(k), :]).then_inc(x_loaded[k], 16)
                if k == 0:
                    sp.dma_start(wk[:], wk_aug).then_inc(consts_loaded, 16)
                    sp.dma_start(wv[:], wv_aug).then_inc(consts_loaded, 16)
                    sp.dma_start(wo[:], wo_t).then_inc(consts_loaded, 16)
                    sp.dma_start(bo[:], b_o).then_inc(consts_loaded, 16)
                    sp.dma_start(router_raw[0:C, :], router_t).then_inc(consts_loaded, 16)
                    sp.dma_start(router_raw[C:P, :], router_t).then_inc(consts_loaded, 16)
            for q in range(PAIRS):
                r = q % 2
                if q >= 2:
                    sp.wait_ge(w_lo_made, 3 * (q - 1))
                for raw, src in ((w1_raw, w1_t), (w3_raw, w3_t)):
                    for half in range(2):
                        sp.dma_start(raw[C * half:C * half + C, r, :], src[:, q, :]).then_inc(raw_loaded[r], 16)
                sp.dma_start(w2_raw[:, r, :, :], w2_t[:, q, :, :]).then_inc(raw_loaded[r], 16)
            with sp.Fori(0, NBLK - 1) as blk:
                sp.wait_ge(bank6_read, blk * 2 + 3)
                sp.dma_start(out[:, bass.ds(blk * BPB, BPB), :],
                             tT[:, bass.ds(blk * BLK, BLK)].rearrange("c (b n) -> c b n", n=N)).then_inc(stored, 16)
            sp.wait_ge(bank6_read, 2 * NBLK)
            sp.dma_start(out[:, BPB * (NBLK - 1):, :],
                         tT[:, cols(NBLK - 1)].rearrange("c (b n) -> c b n", n=N)).then_inc(stored, 16)
            sp.wait_ge(stored, 16 * NBLK)

        @block.gpsimd
        def _(pool):
            nc.gpsimd.memset(ident[:], 0.0).then_inc(pool_step, 1)
            nc.gpsimd.memset(earlier[:], 1.0).then_inc(pool_step, 1)
            nc.gpsimd.memset(last_row[:], 0.0).then_inc(pool_step, 1)
            nc.gpsimd.memset(neg_half[:], -0.5).then_inc(consts_made, 1)
            pool.wait_ge(pool_step, 3)
            nc.gpsimd.affine_select(out=ident[:], in_=ident[:], compare_op=ALU.not_equal, fill=1.0, base=0,
                                    pattern=[[-1, P]], channel_multiplier=1).then_inc(consts_made, 1)
            nc.gpsimd.affine_select(out=earlier[:], in_=earlier[:], compare_op=ALU.is_gt, fill=0.0, base=0,
                                    pattern=[[1, E], [-1, E]], channel_multiplier=0).then_inc(consts_made, 1)
            nc.gpsimd.memset(last_row[:, C:C + 1], 1.0).then_inc(consts_made, 1)

            def inverse_deviation(norm, k):
                n = norm * TPB + 0
                pool.wait_ge(var_ready, ORDER.index((norm, k)) + 1)
                nc.gpsimd.tensor_tensor(rstd[:, norm, tiles(k)], var[:, norm, tiles(k)], neg_half[:, 0:TPB],
                                        ALU.pow).then_inc(rstd_ready, 1)

            def split_low(q):
                r = q % 2
                pool.wait_ge(raw_loaded[r], 16 * RAW_DMAS * (q // 2 + 1))
                pool.wait_ge(rstd_ready, ORDER.index((1, q)) + 1)
                for i, (raw, split) in enumerate(((w1_raw, w1_split), (w3_raw, w3_split))):
                    pool.wait_ge(w_hi_made, 3 * q + i + 1)
                    lo = split[C:P, q, :]
                    nc.gpsimd.tensor_tensor(lo, raw[C:P, r, :], lo.bitcast(F32), ALU.subtract).then_inc(w_lo_made, 1)
                pool.wait_ge(w_hi_made, 3 * q + 3)
                pool.wait_ge(w_lo_made, 3 * q + 2)
                part = slice(2 * SLOTS * q, 2 * SLOTS * (q + 1))
                nc.gpsimd.tensor_tensor(w2_split[:, part, 1, :], w2_raw[:, r, :, :],
                                        w2_split[:, part, 0, :].bitcast(F32), ALU.subtract).then_inc(w_lo_made, 1)

            pool.wait_ge(consts_made, 4)
            for i, (norm, k) in enumerate(ORDER):
                inverse_deviation(norm, k)
                if norm:
                    split_low(k)

            def tick(base, place, first, tail):
                s = place % STEPS
                if s in DVE_LO or tail:
                    return
                n = step_no(base, place)
                pool.wait_ge(hid_hi_made, n + 1)
                if not (first and place < RING):
                    pool.wait_ge(hid_used, n - RING + 1)
                nc.gpsimd.tensor_tensor(hid_lo[:, s % RING, :], hid[:, s % RING, :],
                                        hid_hi[:, s % RING, :].bitcast(F32), ALU.subtract).then_inc(hid_lo_pool, 1)

            run_blocks(pool, tick)

        @block.scalar
        def _(act):
            def xT_copy(k):
                act.wait_ge(xT_done, k + 1)
                if k >= 2:
                    act.wait_ge(u_done, k - 1)
                nc.scalar.copy(xT[0:C, k % 2, :], bank[6][0:C, :]).then_inc(xT_copied, 1)

            def kq_copy(k):
                act.wait_ge(kq_done, k + 1)
                if k >= 2:
                    act.wait_ge(sim_done, BPB * (k - 1))
                nc.scalar.copy(kq[:, k % 2, :], bank[7][0:CK, :]).then_inc(kq_copied, 1)

            def exponentials(b):
                act.wait_ge(max_ready, b + 1)
                if b >= 2:
                    act.wait_ge(probsT_done, b - 1)
                for i in range(2):
                    nc.scalar.activation(probs[:, b % 2, i, :], S_BANK[b % 2][:, N * i:N * (i + 1)], ACT.Exp,
                                         bias=neg_max[:, b, i:i + 1]).then_inc(probs_ready, 1)

            def probsT_copy(b):
                act.wait_ge(probsT_done, b + 1)
                if b >= 2:
                    act.wait_ge(attn_done, b - 1)
                nc.scalar.copy(probsT[:, b % 2, :, :], PT_BANK[b % 2][:]).then_inc(probsT_copied[1], 1)

            def t_high(k):
                act.wait_ge(tnT_done, k + 1)
                nc.scalar.copy(t_hi[:, cols(k)], bank[7][:]).then_inc(hi_ready, 1)

            def tT_copy(k):
                act.wait_ge(tT_done, k + 1)
                nc.scalar.copy(tT[:, cols(k)], bank[6][0:C, :]).then_inc(tT_copied, 1)

            def split_high(q):
                r = q % 2
                act.wait_ge(raw_loaded[r], 16 * RAW_DMAS * (q // 2 + 1))
                nc.scalar.copy(w1_split[:, q, :], w1_raw[:, r, :]).then_inc(w_hi_made, 1)
                nc.scalar.copy(w3_split[:, q, :], w3_raw[:, r, :]).then_inc(w_hi_made, 1)
                nc.scalar.copy(w2_split[:, 2 * SLOTS * q:2 * SLOTS * (q + 1), 0, :],
                               w2_raw[:, r, :, :]).then_inc(w_hi_made, 1)

            xT_copy(0)
            kq_copy(0)
            for k in range(NBLK + 1):
                if k < NBLK:
                    exponentials(BPB * k)
                    exponentials(BPB * k + 1)
                if k + 1 < NBLK:
                    xT_copy(k + 1)
                    kq_copy(k + 1)
                if k >= 1:
                    t_high(k - 1)
                    tT_copy(k - 1)
                if k < NBLK:
                    probsT_copy(BPB * k + 1)
                    split_high(k)
            act.wait_ge(shifted, 1)
            nc.scalar.activation(expo[:], picked[:], ACT.Exp).then_inc(exponents, 1)

            def tick(base, place, first, tail):
                s = place % STEPS
                n = step_no(base, place)
                if not tail:
                    act.wait_ge(h1_done, n + 1)
                    if not (first and place < 2):
                        act.wait_ge(hid_done, n - 1)
                    nc.scalar.activation(act_sb[:, s % 2, :], H1_BANK[s % 2][:], ACT.Silu).then_inc(silu_done, 1)
                if place >= 1 and place <= STEPS or not tail and not (first and place == 0):
                    r = (s - 1) % RING
                    act.wait_ge(hid_done, n)
                    if not (first and place < RING + 1):
                        act.wait_ge(hid_used, n - RING)
                    nc.scalar.copy(hid_hi[:, r, :], hid[:, r, :]).then_inc(hid_hi_made, 1)
                if s in SPREAD_COPY_AT and not tail:
                    e = SPREAD_COPY_AT[s]
                    ee = base * E + E * (place // STEPS) + e
                    act.wait_ge(spread_done, ee + 1)
                    if not (first and e < 2):
                        act.wait_ge(y_gated, ee - 1)
                    nc.scalar.copy(gate_b[:, e % 2, :], bank[7][:]).then_inc(spread_copied, 1)

            run_blocks(act, tick)

        @block.vector
        def _(dve):
            steps = [0]

            def chain(ins):
                steps[0] += 1
                ins.then_inc(dve_step, 1)
                dve.wait_ge(dve_step, steps[0])

            def statistics(norm, k, src):
                chain(nc.vector.tensor_reduce(mean[:], src, AX.X, ALU.add))
                chain(nc.vector.tensor_scalar(mean[:], mean[:], 1.0 / C, None, ALU.mult))
                chain(nc.vector.tensor_tensor(cent[:], src, mean[:].unsqueeze(2).to_broadcast([P, TPB, C]),
                                              ALU.subtract))
                chain(nc.vector.tensor_tensor(sq[:], cent[:], cent[:], ALU.mult))
                chain(nc.vector.tensor_reduce(ssq[:], sq[:], AX.X, ALU.add))
                nc.vector.tensor_scalar(var[:, norm, tiles(k)], ssq[:], 1.0 / C, 1e-5 if norm else 1e-6,
                                        ALU.mult, ALU.add).then_inc(var_ready, 1)

            def normalise_x(k):
                dve.wait_ge(x_loaded[k], 16)
                statistics(0, k, x_sb[:, tiles(k), :])
                dve.wait_ge(rstd_ready, ORDER.index((0, k)) + 1)
                nc.vector.tensor_tensor(xn[:, tiles(k), :], cent[:],
                                        rstd[:, 0, tiles(k)].unsqueeze(2).to_broadcast([P, TPB, C]),
                                        ALU.mult).then_inc(xn_ready, 1)
                dve.wait_ge(xn_ready, k + 1)

            def normalise_t(k):
                dve.wait_ge(t_ready, TPB * (k + 1))
                statistics(1, k, t_sb[:, tiles(k), :])
                dve.wait_ge(rstd_ready, ORDER.index((1, k)) + 1)
                if k >= 2:
                    dve.wait_ge(tnT_done, k - 1)
                for half in range(2):
                    ins = nc.vector.tensor_tensor(tn[:, k % 2, :, half, :], cent[:],
                                                  rstd[:, 1, tiles(k)].unsqueeze(2).to_broadcast([P, TPB, C]),
                                                  ALU.mult)
                    ins.then_inc(tn_ready, 1)
                dve.wait_ge(tn_ready, 2 * (k + 1))

            def u_copy(k):
                dve.wait_ge(u_done, k + 1)
                nc.vector.tensor_copy(u_sb[:, tiles(k), :],
                                      bank[6][:, 0:TPB * (C + 1)].rearrange("p (t c) -> p t c", c=C + 1)
                                      ).then_inc(u_copied, 1)

            def row_max(b):
                dve.wait_ge(sim_done, b + 1)
                nc.vector.tensor_reduce(neg_max[:, b, :], S_BANK[b % 2][:].rearrange("p (i n) -> p i n", n=N),
                                        AX.X, ALU.max, negate=True).then_inc(max_ready, 1)

            def probsT_copy(b):
                dve.wait_ge(probsT_done, b + 1)
                if b >= 2:
                    dve.wait_ge(attn_done, b - 1)
                nc.vector.tensor_copy(probsT[:, b % 2, :, :], PT_BANK[b % 2][:].rearrange("p (j n) -> p j n", n=N)
                                      ).then_inc(probsT_copied[0], 1)

            def residual(b):
                o = O_BANK[b % 2][:, 0:2 * (C + 1)].rearrange("p (i c) -> p i c", c=C + 1)
                dve.wait_ge(attn_done, b + 1)
                nc.vector.reciprocal(inv_sum[:, b, :], o[:, :, C]).then_inc(sum_inverted, 1)
                dve.wait_ge(sum_inverted, b + 1)
                for i in range(2):
                    nc.vector.scalar_tensor_tensor(out=t_sb[:, 2 * b + i, :], in0=o[:, i, 0:C],
                                                   scalar=inv_sum[:, b, i:i + 1], in1=x_sb[:, 2 * b + i, :],
                                                   op0=ALU.mult, op1=ALU.add).then_inc(t_ready, 1)

            def t_low(k):
                dve.wait_ge(hi_ready, k + 1)
                nc.vector.tensor_tensor(t_lo[:, cols(k)], bank[7][:], t_hi[:, cols(k)].bitcast(F32),
                                        ALU.subtract).then_inc(lo_ready, 1)

            def logits_copy(k):
                dve.wait_ge(logits_done, k + 1)
                nc.vector.tensor_copy(logits[:, tiles(k), :],
                                      bank[6][:, 0:TPB * E].rearrange("p (t e) -> p t e", e=E)
                                      ).then_inc(logits_copied, 1)

            nc.vector.memset(xT[C:C + 1, :, :], 1.0).then_inc(dve_consts, 1)
            normalise_x(0)
            normalise_x(1)
            dve.wait_ge(consts_loaded, 16 * CONST_DMAS)
            dve.wait_ge(consts_made, 4)
            chain(nc.vector.tensor_copy(router[:], router_raw[:]))
            nc.vector.tensor_tensor(router[C:P, :], router_raw[C:P, :], router[C:P, :].bitcast(F32),
                                    ALU.subtract).then_inc(dve_consts, 1)
            nc.vector.tensor_tensor(pick_gate[:], ident[0:2 * E, 0:E].unsqueeze(2).to_broadcast([2 * E, E, P]),
                                    ident[0:2 * E, E:2 * E].unsqueeze(2).to_broadcast([2 * E, E, P]),
                                    ALU.add).then_inc(dve_consts, 1)
            nc.vector.tensor_tensor(fold[:], ident[:, 0:C], ident[:, C:P], ALU.add).then_inc(dve_consts, 1)
            dve.wait_ge(wu_done, 1)
            nc.vector.tensor_copy(wu[:, 0:C], bank[5][0:C + 1, 0:C]).then_inc(wu_copied, 1)
            nc.vector.tensor_copy(wu[:, C:C + 1], ident[0:C + 1, C:C + 1]).then_inc(wu_copied, 1)
            u_copy(0)
            for k in range(NBLK + 1):
                if k < NBLK:
                    row_max(BPB * k)
                    row_max(BPB * k + 1)
                if k + 1 < NBLK:
                    u_copy(k + 1)
                if k >= 1:
                    t_low(k - 1)
                    logits_copy(k - 1)
                if k < NBLK:
                    probsT_copy(BPB * k)
                    residual(BPB * k)
                    residual(BPB * k + 1)
                    if k + 2 < NBLK:
                        normalise_x(k + 2)
                    normalise_t(k)
            top, total, chosen, share = (small[:, i, :] for i in range(4))
            per_e = lambda v: v.unsqueeze(2).to_broadcast([P, TILES, E])
            dve.wait_ge(logits_copied, NBLK)
            chain(nc.vector.tensor_reduce(top, logits[:], AX.X, ALU.max))
            nc.vector.tensor_tensor(picked[:], logits[:], per_e(top), ALU.subtract).then_inc(shifted, 1)
            other = logits[:].unsqueeze(2).to_broadcast([P, TILES, E, E])
            own = logits[:].unsqueeze(3).to_broadcast([P, TILES, E, E])
            nc.vector.tensor_tensor(cmp_gt, other, own, ALU.is_gt).then_inc(dve_step, 1)
            chain(nc.vector.tensor_tensor(cmp_eq, other, own, ALU.is_equal))
            steps[0] += 1
            dve.wait_ge(dve_step, steps[0])
            chain(nc.vector.tensor_tensor(cmp_eq, cmp_eq, earlier[:].unsqueeze(1).to_broadcast([P, TILES, E, E]),
                                          ALU.mult))
            chain(nc.vector.tensor_tensor(cmp_gt, cmp_gt, cmp_eq, ALU.add))
            dve.wait_ge(exponents, 1)
            chain(nc.vector.tensor_reduce(picked[:], cmp_gt, AX.X, ALU.add))
            chain(nc.vector.scalar_tensor_tensor(out=picked[:], in0=picked[:], scalar=2.0, in1=expo[:],
                                                 op0=ALU.is_lt, op1=ALU.mult))
            nc.vector.tensor_reduce(chosen, picked[:], AX.X, ALU.add).then_inc(dve_step, 1)
            steps[0] += 1
            chain(nc.vector.tensor_reduce(total, expo[:], AX.X, ALU.add))
            chain(nc.vector.scalar_tensor_tensor(out=share, in0=total, scalar=1e-9, in1=chosen,
                                                 op0=ALU.mult, op1=ALU.add))
            chain(nc.vector.reciprocal(share, share))
            chain(nc.vector.tensor_tensor(picked[:], picked[:], per_e(share), ALU.mult))
            chain(nc.vector.tensor_copy(gates[:, :, 0, :], picked[:]))
            nc.vector.tensor_tensor(gates[:, :, 1, :], picked[:], gates[:, :, 0, :].bitcast(F32),
                                    ALU.subtract).then_inc(gates_ready, 1)
            dve.wait_ge(gates_ready, 1)

            def tick(base, place, first, tail):
                blk, s = divmod(place, STEPS)
                n = step_no(base, place)
                if s == 0 and not tail:
                    if not first:
                        dve.wait_ge(gateT_done, base + blk)
                    nc.vector.tensor_copy(gate_stage[:].rearrange("p t (h e) -> p t h e", e=E),
                                          gates[:, bass.ds((base + blk) * TPB, TPB), :, :].bitcast(F32)
                                          ).then_inc(stage_copied, 1)
                if not tail:
                    dve.wait_ge(silu_done, n + 1)
                    dve.wait_ge(h3_done, n + 1)
                    if not (first and place < RING):
                        dve.wait_ge(hid_hi_made, n - RING + 1)
                        lo_wait(dve, base, place - RING)
                    nc.vector.tensor_tensor(hid[:, s % RING, :], H3_BANK[s % 2][:], act_sb[:, s % 2, :],
                                            ALU.mult).then_inc(hid_done, 1)
                if s == 2 and not tail:
                    dve.wait_ge(gateT_done, base + blk + 1)
                    if not first:
                        dve.wait_ge(spread_done, (base + blk) * E)
                    nc.vector.tensor_copy(gateT[:], bank[6][0:2 * E, :]).then_inc(bank6_read, 1)
                s2 = (s - 2) % STEPS
                if s2 in DVE_LO and not (first and place < 2) and place - 2 < (STEPS if tail else 2 * STEPS):
                    dve.wait_ge(hid_hi_made, n - 1)
                    if not (first and place - 2 < RING):
                        dve.wait_ge(hid_used, n - 2 - RING + 1)
                    nc.vector.tensor_tensor(hid_lo[:, s2 % RING, :], hid[:, s2 % RING, :],
                                            hid_hi[:, s2 % RING, :].bitcast(F32), ALU.subtract
                                            ).then_inc(hid_lo_dve, 1)
                if s in GATE_AT:
                    e, late = GATE_AT[s]
                    of = blk - late
                    if of >= 0 and not (tail and of > 0):
                        ee = base * E + of * E + e
                        dve.wait_ge(hid_used, step_no(base, of * STEPS + LAST[e]) + 1)
                        dve.wait_ge(spread_copied, ee + 1)
                        if e == 0:
                            if not first:
                                dve.wait_ge(fold_done, base + of)
                            nc.vector.tensor_tensor(acc[:], Y_BANK[e % 2][:], gate_b[:, e % 2, :],
                                                    ALU.mult).then_inc(y_gated, 1)
                        else:
                            nc.vector.tensor_tensor(gated[:], Y_BANK[e % 2][:], gate_b[:, e % 2, :],
                                                    ALU.mult).then_inc(y_gated, 1)
                            dve.wait_ge(y_gated, ee + 1)
                            if e > 1:
                                dve.wait_ge(acc_added, (base + of) * (E - 1) + e - 1)
                            nc.vector.tensor_tensor(acc[:], acc[:], gated[:], ALU.add).then_inc(acc_added, 1)
                if s == RESULT_AT and not first and not (tail and blk == 0):
                    dve.wait_ge(fold_done, base + blk)
                    res = tT[:, bass.ds((base + blk - 1) * BLK, BLK)]
                    nc.vector.tensor_tensor(res, bank[6][0:C, :], res, ALU.add).then_inc(bank6_read, 1)

            run_blocks(dve, tick)

        @block.tensor
        def _(pe):
            def transpose_x(k):
                pe.wait_ge(xn_ready, k + 1)
                if k >= 3:
                    pe.wait_ge(logits_copied, k - 2)
                if k >= 1:
                    pe.wait_ge(u_copied, k)
                for t in range(TPB):
                    ins = nc.tensor.transpose(bank[6][0:C, P * t:P * (t + 1)], xn[:, TPB * k + t, :], ident[:])
                ins.then_inc(xT_done, 1)

            def key_query(k):
                pe.wait_ge(xT_copied, k + 1)
                if k >= 1:
                    pe.wait_ge(kq_copied, k)
                if k >= 3:
                    pe.wait_ge(lo_ready, k - 2)
                nc.tensor.matmul(bank[7][0:CK, :], wk[:], xT[:, k % 2, :], start=True, stop=True).then_inc(kq_done, 1)

            def value_out(k):
                if k == 0:
                    pe.wait_ge(wu_copied, 2)
                pe.wait_ge(xT_copied, k + 1)
                for t in range(TPB):
                    ins = nc.tensor.matmul(bank[6][:, (C + 1) * t:(C + 1) * (t + 1)], xT[:, k % 2, P * t:P * (t + 1)],
                                           wu[:], start=True, stop=True)
                ins.then_inc(u_done, 1)

            def similarity(b):
                k, i0 = b // BPB, N * (b % BPB)
                pe.wait_ge(kq_copied, k + 1)
                if b >= 2:
                    pe.wait_ge(probs_ready, 2 * (b - 1))
                for i in range(2):
                    ins = nc.tensor.matmul(S_BANK[b % 2][:, N * i:N * (i + 1)],
                                           kq[:, k % 2, i0 + P * i:i0 + P * (i + 1)], kq[:, k % 2, i0:i0 + N],
                                           start=True, stop=True)
                ins.then_inc(sim_done, 1)

            def transpose_probs(b):
                pe.wait_ge(probs_ready, 2 * (b + 1))
                if b >= 2:
                    pe.wait_ge(probsT_copied[b % 2], b // 2)
                for i in range(2):
                    for j in range(2):
                        ins = nc.tensor.transpose(PT_BANK[b % 2][:, N * j + P * i:N * j + P * (i + 1)],
                                                  probs[:, b % 2, i, P * j:P * (j + 1)], ident[:])
                ins.then_inc(probsT_done, 1)

            def attend(b):
                pe.wait_ge(probsT_copied[b % 2], b // 2 + 1)
                pe.wait_ge(u_copied, b // BPB + 1)
                if b >= 2:
                    pe.wait_ge(t_ready, 2 * (b - 1))
                for i in range(2):
                    for j in range(2):
                        ins = nc.tensor.matmul(O_BANK[b % 2][:, (C + 1) * i:(C + 1) * (i + 1)],
                                               probsT[:, b % 2, j, P * i:P * (i + 1)], u_sb[:, 2 * b + j, :],
                                               start=(j == 0), stop=(j == 1))
                ins.then_inc(attn_done, 1)

            def transpose_t(k):
                pe.wait_ge(tn_ready, 2 * (k + 1))
                pe.wait_ge(kq_copied, min(k + 3, NBLK))
                pe.wait_ge(u_copied, min(k + 3, NBLK))
                if k >= 1:
                    pe.wait_ge(lo_ready, k)
                    pe.wait_ge(logits_copied, k)
                for t in range(TPB):
                    ins = nc.tensor.transpose(bank[7][:, P * t:P * (t + 1)],
                                              tn[:, k % 2, t, :, :], ident[:])
                ins.then_inc(tnT_done, 1)
                for t in range(TPB):
                    ins = nc.tensor.transpose(bank[6][0:C, P * t:P * (t + 1)], t_sb[:, TPB * k + t, :], ident[:])
                ins.then_inc(tT_done, 1)

            def route(k):
                pe.wait_ge(tT_copied, k + 1)
                pe.wait_ge(hi_ready, k + 1)
                pe.wait_ge(lo_ready, k + 1)
                pe.wait_ge(dve_consts, 2)
                for t in range(TPB):
                    own = slice(BLK * k + P * t, BLK * k + P * (t + 1))
                    for part, ends in ((t_hi, (True, False)), (t_lo, (False, True))):
                        ins = nc.tensor.matmul(bank[6][:, E * t:E * (t + 1)], part[:, own], router[:],
                                               start=ends[0], stop=ends[1])
                ins.then_inc(logits_done, 1)

            pe.wait_ge(consts_loaded, 16 * CONST_DMAS)
            pe.wait_ge(consts_made, 4)
            nc.tensor.matmul(bank[5][0:C + 1, 0:C], wv[:], wo[:], start=True, stop=False)
            nc.tensor.matmul(bank[5][0:C + 1, 0:C], last_row[:], bo[:], start=False, stop=True).then_inc(wu_done, 1)
            transpose_x(0)
            pe.wait_ge(dve_consts, 1)
            key_query(0)
            value_out(0)
            for k in range(NBLK + 1):
                if k < NBLK:
                    similarity(BPB * k)
                    similarity(BPB * k + 1)
                if k + 1 < NBLK:
                    transpose_x(k + 1)
                    key_query(k + 1)
                    value_out(k + 1)
                if k >= 1:
                    transpose_t(k - 1)
                    route(k - 1)
                if k < NBLK:
                    for b in range(BPB * k, BPB * (k + 1)):
                        transpose_probs(b)
                    for b in range(BPB * k, BPB * (k + 1)):
                        attend(b)

            def up(base, place, first):
                blk, s = divmod(place, STEPS)
                n = step_no(base, place)
                q, j = divmod(s, CHUNKS)
                if place < STEPS and j == 0 and (first or base is NBLK - 1 or True):
                    pe.wait_ge(w_hi_made, 3 * (q + 1))
                    pe.wait_ge(w_lo_made, 3 * (q + 1))
                own = bass.ds((base + blk) * BLK, BLK)
                for split, banks, freed, done in ((w1_split, H1_BANK, silu_done, h1_done),
                                                  (w3_split, H3_BANK, hid_done, h3_done)):
                    w = split[:, q, P * j:P * (j + 1)]
                    if not (first and place < 2):
                        pe.wait_ge(freed, n - 1)
                    nc.tensor.matmul(banks[s % 2][:], w, t_hi[:, own], start=True, stop=False)
                    nc.tensor.matmul(banks[s % 2][:], w, t_lo[:, own], start=False, stop=True).then_inc(done, 1)

            def down(base, place, first):
                blk, s = divmod(place, STEPS)
                q, j = divmod(s, CHUNKS)
                pe.wait_ge(hid_hi_made, step_no(base, place) + 1)
                lo_wait(pe, base, place)
                slots = ([(0, j)] if j <= SEAM else []) + ([(1, j - SEAM)] if j >= SEAM else [])
                for side, slot in slots:
                    if slot == 0 and not (first and q == 0):
                        pe.wait_ge(y_gated, (base + blk) * E + 2 * q + side - 1)
                    w = w2_split[:, 2 * SLOTS * q + SLOTS * side + slot, :, :]
                    nc.tensor.matmul(Y_BANK[side][:], w, hid_hi[:, s % RING, :], start=(slot == 0), stop=False)
                    ins = nc.tensor.matmul(Y_BANK[side][:], w, hid_lo[:, s % RING, :], start=False,
                                           stop=(slot == SEAM))
                ins.then_inc(hid_used, 1)

            def tick(base, place, first, tail):
                blk, s = divmod(place, STEPS)
                if not tail:
                    up(base, place, first)
                if s == 1 and not tail:
                    pe.wait_ge(stage_copied, base + blk + 1)
                    if not first:
                        pe.wait_ge(bank6_read, (base + blk) * 2 - 1)
                    for t in range(TPB):
                        ins = nc.tensor.transpose(bank[6][0:2 * E, P * t:P * (t + 1)], gate_stage[:, t, :], ident[:])
                    ins.then_inc(gateT_done, 1)
                if s in SPREAD_AT and not tail:
                    e = SPREAD_AT[s]
                    ee = base * E + blk * E + e
                    if e == 0:
                        pe.wait_ge(bank6_read, 1 if first else (base + blk) * 2)
                    if not (first and e == 0):
                        pe.wait_ge(spread_copied, ee)
                    nc.tensor.matmul(bank[7][:], pick_gate[:, e, :], gateT[:], start=True,
                                     stop=True).then_inc(spread_done, 1)
                if place >= LAG and (not tail or place - LAG < STEPS):
                    down(base, place - LAG, first)
                if s == FOLD_AT and not first and not (tail and blk == 0):
                    pe.wait_ge(acc_added, (base + blk) * (E - 1))
                    pe.wait_ge(bank6_read, (base + blk) * 2 - (1 if tail else 0))
                    nc.tensor.matmul(bank[6][0:C, :], fold[:], acc[:], start=True, stop=True).then_inc(fold_done, 1)

            pe.wait_ge(dve_consts, 4)
            run_blocks(pe, tick)


ORDER = [(0, 0), (0, 1)] + [p for k in range(NBLK) for p in ([(0, k + 2)] if k + 2 < NBLK else []) + [(1, k)]]


def kernel(**inputs):
    import numpy as np
    import concourse.bacc as bacc
    from concourse.bass_utils import run_bass_kernel_spmd

    a = {k: np.asarray(v) for k, v in inputs.items()}

    def experts(w):
        w = w.reshape(PAIRS, 2 * H, C).transpose(2, 0, 1)
        return np.concatenate([w, np.zeros((C, PAIRS, PW - 2 * H), w.dtype)], axis=2)

    w2 = np.zeros((PAIRS, 2, SLOTS * P, C), a["L0_ffn_w2"].dtype)
    rows = a["L0_ffn_w2"].transpose(0, 2, 1).reshape(PAIRS, 2, H, C)
    w2[:, 0, 0:H] = rows[:, 0]
    at = H - SEAM * P
    w2[:, 1, at:at + H] = rows[:, 1]
    arrays = {
        "x_tok": a["x"].reshape(B, C, N // P, P).transpose(3, 0, 2, 1).reshape(P, TILES, C),
        "wk_aug": np.concatenate([a["L0_conv_w_kq"].T, a["L0_conv_b_kq"][None]], axis=0),
        "wv_aug": np.concatenate([a["L0_conv_w_v"], a["L0_conv_b_v"][:, None]], axis=1),
        "wo_t": a["L0_conv_w_o"].T,
        "b_o": a["L0_conv_b_o"][None],
        "router_t": a["L0_ffn_router_w"].T,
        "w1_t": experts(a["L0_ffn_w1"]),
        "w3_t": experts(a["L0_ffn_w3"]),
        "w2_t": w2.reshape(PAIRS, 2 * SLOTS, P, C).transpose(2, 0, 1, 3),
    }
    arrays = {k: np.ascontiguousarray(v) for k, v in arrays.items()}
    nc = bacc.Bacc("TRN2", target_bir_lowering=False, num_devices=1)
    args = [nc.dram_tensor(k, v.shape, F32, kind="ExternalInput").ap() for k, v in arrays.items()]
    out = nc.dram_tensor("out", (B, C, N), F32, kind="ExternalOutput").ap()
    metaformer(nc, *args, out.rearrange("b c n -> c b n"))
    got = run_bass_kernel_spmd(nc, [arrays], core_ids=[0]).results[0]["out"]
    return got.reshape(B, C, 16, 16)
```

```python
from contextlib import ExitStack

import concourse.bass as bass
from concourse import mybir

F32 = mybir.dt.float32
F32R = mybir.dt.float32r
ALU = mybir.AluOpType
ACT = mybir.ActivationFunctionType
AX = mybir.AxisListType

B, C, N = 8, 64, 256
CK = 32
E, H = 8, 682
P = 128
TILES = B * N // P
BLK = 512
NBLK = B * N // BLK
TPB = BLK // P
BPB = BLK // N
PAIRS = E // 2
CHUNKS = -(-2 * H // P)
SEAM = H // P
SLOTS = SEAM + 1
PW = CHUNKS * P
STEPS = PAIRS * CHUNKS
LAG = 4
RING = 4
ROT = 16
DVE_LO = (6, 11, 16, 22, 27, 33, 38)


def metaformer(nc, x_tok, wk_t, b_kq, w_v, b_v, wo_t, b_o, router_t, w1_t, w3_t, w2_t, out):
    with ExitStack() as ctx:
        def sb(name, shape, dt=F32):
            return ctx.enter_context(nc.sbuf_tensor(name, shape, dt))

        def sem(name):
            return ctx.enter_context(nc.semaphore(name))

        bank = [ctx.enter_context(nc.psum_tensor(f"bank{i}", [P, BLK], F32)) for i in range(8)]

        ident = sb("ident", [P, P])
        order_val = sb("order_val", [P, E])
        neg_half = sb("neg_half", [P, TILES])
        ones_row = sb("ones_row", [1, P])
        pick_gate = sb("pick_gate", [2 * E, E, P], F32R)
        fold = sb("fold", [P, C])
        w1_raw = sb("w1_raw", [P, 2, PW])
        w3_raw = sb("w3_raw", [P, 2, PW])
        w2_raw = sb("w2_raw", [P, 2, 2 * SLOTS, C])
        w1_split = sb("w1_split", [P, PAIRS, PW], F32R)
        w3_split = sb("w3_split", [P, PAIRS, PW], F32R)
        w2_split = sb("w2_split", [P, PAIRS * 2 * SLOTS, 2, C], F32R)
        wk_raw = sb("wk_raw", [P, CK])
        wk = sb("wk", [P, CK], F32R)
        bk = sb("bk", [CK, 1])
        wv = sb("wv", [CK, 2, C])
        bv = sb("bv", [CK, 1])
        wo = sb("wo", [CK, C])
        bo = sb("bo", [1, C])
        wu = sb("wu", [P, C], F32R)
        router_raw = sb("router_raw", [P, E])
        router = sb("router", [P, E], F32R)
        x_sb = sb("x_sb", [P, TILES, C])
        x_bias = sb("x_bias", [P, TILES, C])
        t_sb = sb("t_sb", [P, TILES, C])
        tn = sb("tn", [P, 2, TPB, 2, C])
        cent = sb("cent", [P, TILES, C])
        sq = sb("sq", [P, TILES, C])
        mean = sb("mean", [P, TILES])
        ssq = sb("ssq", [P, TILES])
        var = sb("var", [P, 2, TILES])
        rstd = sb("rstd", [P, 2, TILES])
        t_hi = sb("t_hi", [P, NBLK * BLK], F32R)
        t_lo = sb("t_lo", [P, NBLK * BLK], F32R)
        tT = sb("tT", [C, NBLK * BLK])
        u_sb = sb("u_sb", [P, TILES, C + 1])
        neg_max = sb("neg_max", [P, B, 2])
        bias = sb("bias", [P, C])
        inv_sum = sb("inv_sum", [P, B, 2])
        logits = sb("logits", [P, TILES, E])
        probsT = sb("probsT", [P, 2, 2, N])
        small = sb("small", [P, 6, TILES])
        is_top = sb("is_top", [P, 2, TILES, E])
        rest = sb("rest", [P, TILES, E])
        expo = sb("expo", [P, TILES, E])
        picked = sb("picked", [P, TILES, E])
        t_stage = sb("t_stage", [P, TPB, 2, C])
        gates = sb("gates", [P, TILES, 2, E], F32R)
        gate_stage = sb("gate_stage", [P, TPB, 2 * E])
        gateT = sb("gateT", [2 * E, BLK], F32R)
        act_sb = sb("act_sb", [P, 2, BLK])
        hid = sb("hid", [P, RING, BLK])
        hid_hi = sb("hid_hi", [P, RING, BLK], F32R)
        hid_lo = sb("hid_lo", [P, RING, BLK], F32R)
        gate_b = sb("gate_b", [P, 2, BLK])
        gated = sb("gated", [P, BLK])
        acc = sb("acc", [P, BLK])
        x_hi = t_hi[:].rearrange("p (k n) -> p k n", n=BLK)
        x_lo = t_lo[:].rearrange("p (k n) -> p k n", n=BLK)
        probs = act_sb[:].rearrange("p r (i n) -> p r i n", n=N)
        kq_hi, kq_lo = hid_hi[0:CK, 2:4, :], hid_lo[0:CK, 2:4, :]
        xn = hid[:].rearrange("p r (t h c) -> p (r t) h c", h=2, c=C)

        x_loaded = [sem(f"x_loaded{k}") for k in range(NBLK)]
        consts_loaded = sem("consts_loaded")
        raw_loaded = [sem("raw_loaded0"), sem("raw_loaded1")]
        stored = sem("stored")
        consts_made = sem("consts_made")
        pool_step = sem("pool_step")
        dve_step = sem("dve_step")
        dve_consts = sem("dve_consts")
        var_ready = sem("var_ready")
        rstd_ready = sem("rstd_ready")
        xn_ready = sem("xn_ready")
        xT_done, x_hi_ready, x_lo_ready = sem("xT_done"), sem("x_hi_ready"), sem("x_lo_ready")
        kq_done, kq_hi_ready, kq_lo_ready = sem("kq_done"), sem("kq_hi_ready"), sem("kq_lo_ready")
        u_done, u_copied = sem("u_done"), sem("u_copied")
        wu_done, bias_done, bias_added = sem("wu_done"), sem("bias_done"), sem("bias_added")
        bias_copied = sem("bias_copied")
        sim_done = sem("sim_done")
        max_ready = sem("max_ready")
        probs_ready = sem("probs_ready")
        probsT_done = sem("probsT_done")
        probsT_copied = [sem("probsT_copied_dve"), sem("probsT_copied_act")]
        attn_done = sem("attn_done")
        sum_inverted = sem("sum_inverted")
        t_ready = sem("t_ready")
        tn_ready = sem("tn_ready")
        tnT_done = sem("tnT_done")
        hi_ready, lo_ready = sem("t_hi_ready"), sem("t_lo_ready")
        t_staged = sem("t_staged")
        tT_done, tT_copied = sem("tT_done"), sem("tT_copied")
        logits_done, logits_copied = sem("logits_done"), sem("logits_copied")
        shifted, exponents = sem("shifted"), sem("exponents")
        gates_ready = sem("gates_ready")
        w_hi_made, w_lo_made = sem("w_hi_made"), sem("w_lo_made")
        h1_done, h3_done = sem("h1_done"), sem("h3_done")
        silu_done = sem("silu_done")
        hid_done = sem("hid_done")
        hid_hi_made = sem("hid_hi_made")
        hid_lo_pool, hid_lo_dve = sem("hid_lo_pool"), sem("hid_lo_dve")
        hid_used = sem("hid_used")
        stage_copied = sem("stage_copied")
        gateT_done = sem("gateT_done")
        bank6_read = sem("bank6_read")
        spread_done, spread_copied = sem("spread_done"), sem("spread_copied")
        y_gated = sem("y_gated")
        acc_added = sem("acc_added")
        fold_done = sem("fold_done")

        S_BANK, PT_BANK, O_BANK, U_BANK = bank[0:2], bank[2:4], bank[4], bank[5]
        T_BANK, K_BANK = bank[6], bank[7]
        H1_BANK, H3_BANK, Y_BANK = bank[0:2], bank[2:4], bank[4:6]
        CONST_DMAS = 10
        RAW_DMAS = 5

        def tiles(k):
            return slice(TPB * k, TPB * (k + 1))

        def cols(k):
            return slice(BLK * k, BLK * (k + 1))

        def step_no(base, place):
            return base * STEPS + place

        def lo_wait(eng, base, place):
            blk, s = divmod(place, STEPS)
            n_dve = sum(d < s for d in DVE_LO)
            if s in DVE_LO:
                eng.wait_ge(hid_lo_dve, base * len(DVE_LO) + blk * len(DVE_LO) + n_dve + 1)
            else:
                n_pool = STEPS - len(DVE_LO)
                eng.wait_ge(hid_lo_pool, base * n_pool + blk * n_pool + s - n_dve + 1)

        FIRST = [CHUNKS * (e // 2) + SEAM * (e % 2) for e in range(E)]
        LAST = [f + SEAM for f in FIRST]
        ROUTE_AT = 4
        STAGE_AT = 8
        SPREAD_AT = {max(f + LAG, STAGE_AT + 3 + 2 * e + 2 * (e >= 2)): e for e, f in enumerate(FIRST)}
        SPREAD_COPY_AT = {at + 1: e for at, e in SPREAD_AT.items()}
        TRANSPOSE_T_AT = STAGE_AT + 7
        GATE_AT = {(l + LAG + 1 + (e == 1)) % STEPS: (e, (l + LAG + 1) // STEPS) for e, l in enumerate(LAST) if e}
        GATE_AT[STAGE_AT + 5] = (0, 0)
        FOLD_AT, RESULT_AT = STAGE_AT + 3, STAGE_AT + 4
        TAIL = RESULT_AT + 1

        def run_blocks(eng, tick):
            for place in range(ROT):
                tick(0, place, first=True, tail=False)
            with eng.Fori(0, NBLK - 1) as blk:
                for place in range(ROT, STEPS + ROT):
                    tick(blk, place, first=False, tail=False)
            for place in range(ROT, STEPS + TAIL):
                tick(NBLK - 1, place, first=False, tail=place >= STEPS)

        block = ctx.enter_context(nc.Block())

        @block.sync
        def _(sp):
            for k in range(NBLK):
                sp.dma_start(x_sb[:, tiles(k), :], x_tok[:, tiles(k), :]).then_inc(x_loaded[k], 16)
                if k == 0:
                    sp.dma_start(wk_raw[0:C, :], wk_t).then_inc(consts_loaded, 16)
                    sp.dma_start(wk_raw[C:P, :], wk_t).then_inc(consts_loaded, 16)
                    sp.dma_start(bk[:], b_kq).then_inc(consts_loaded, 16)
                    sp.dma_start(wv[:, 0, :], w_v).then_inc(consts_loaded, 16)
                    sp.dma_start(wv[:, 1, :], w_v).then_inc(consts_loaded, 16)
                    sp.dma_start(bv[:], b_v).then_inc(consts_loaded, 16)
                    sp.dma_start(wo[:], wo_t).then_inc(consts_loaded, 16)
                    sp.dma_start(bo[:], b_o).then_inc(consts_loaded, 16)
                    sp.dma_start(router_raw[0:C, :], router_t).then_inc(consts_loaded, 16)
                    sp.dma_start(router_raw[C:P, :], router_t).then_inc(consts_loaded, 16)
            for q in range(PAIRS):
                r = q % 2
                if q >= 2:
                    sp.wait_ge(w_lo_made, 3 * (q - 1))
                for raw, src in ((w1_raw, w1_t), (w3_raw, w3_t)):
                    for half in range(2):
                        sp.dma_start(raw[C * half:C * half + C, r, :], src[:, q, :]).then_inc(raw_loaded[r], 16)
                sp.dma_start(w2_raw[:, r, :, :], w2_t[:, q, :, :]).then_inc(raw_loaded[r], 16)
            with sp.Fori(0, NBLK - 1) as blk:
                sp.wait_ge(bank6_read, blk * 2 + 3)
                sp.dma_start(out[:, bass.ds(blk * BPB, BPB), :],
                             tT[:, bass.ds(blk * BLK, BLK)].rearrange("c (b n) -> c b n", n=N)).then_inc(stored, 16)
            sp.wait_ge(bank6_read, 2 * NBLK)
            sp.dma_start(out[:, BPB * (NBLK - 1):, :],
                         tT[:, cols(NBLK - 1)].rearrange("c (b n) -> c b n", n=N)).then_inc(stored, 16)
            sp.wait_ge(stored, 16 * NBLK)

        @block.gpsimd
        def _(pool):
            nc.gpsimd.memset(ident[:], 0.0).then_inc(pool_step, 1)
            nc.gpsimd.memset(neg_half[:], -0.5).then_inc(consts_made, 1)
            pool.wait_ge(pool_step, 1)
            nc.gpsimd.affine_select(out=ident[:], in_=ident[:], compare_op=ALU.not_equal, fill=1.0, base=0,
                                    pattern=[[-1, P]], channel_multiplier=1).then_inc(consts_made, 1)
            nc.gpsimd.iota(order_val[:], pattern=[[-1, E]], base=E, channel_multiplier=0, allow_small_or_imprecise_dtypes=True
                          ).then_inc(consts_made, 1)

            def inverse_deviation(n, norm, own):
                pool.wait_ge(var_ready, n + 1)
                nc.gpsimd.tensor_tensor(rstd[:, norm, own], var[:, norm, own], neg_half[:, own],
                                        ALU.pow).then_inc(rstd_ready, 1)

            def split_low(q):
                r = q % 2
                pool.wait_ge(raw_loaded[r], 16 * RAW_DMAS * (q // 2 + 1))
                pool.wait_ge(rstd_ready, 2 + q)
                pool.wait_ge(bias_added, 1)
                for i, (raw, split) in enumerate(((w1_raw, w1_split), (w3_raw, w3_split))):
                    pool.wait_ge(w_hi_made, 3 * q + i + 1)
                    lo = split[C:P, q, :]
                    nc.gpsimd.tensor_tensor(lo, raw[C:P, r, :], lo.bitcast(F32), ALU.subtract).then_inc(w_lo_made, 1)
                pool.wait_ge(w_hi_made, 3 * q + 3)
                pool.wait_ge(w_lo_made, 3 * q + 2)
                part = slice(2 * SLOTS * q, 2 * SLOTS * (q + 1))
                nc.gpsimd.tensor_tensor(w2_split[:, part, 1, :], w2_raw[:, r, :, :],
                                        w2_split[:, part, 0, :].bitcast(F32), ALU.subtract).then_inc(w_lo_made, 1)

            pool.wait_ge(consts_made, 3)
            inverse_deviation(0, 0, tiles(0))
            inverse_deviation(1, 0, slice(TPB, TILES))
            pool.wait_ge(bias_copied, 1)
            nc.gpsimd.tensor_tensor(x_bias[:], x_sb[:], bias[:].unsqueeze(1).to_broadcast([P, TILES, C]),
                                    ALU.add).then_inc(bias_added, 1)
            split_low(0)
            for k in range(NBLK):
                inverse_deviation(2 + k, 1, tiles(k))
                if k + 1 < PAIRS:
                    split_low(k + 1)

            def tick(base, place, first, tail):
                s = place % STEPS
                if s in DVE_LO or tail:
                    return
                n = step_no(base, place)
                pool.wait_ge(hid_hi_made, n + 1)
                if not (first and place < RING):
                    pool.wait_ge(hid_used, n - RING + 1)
                nc.gpsimd.tensor_tensor(hid_lo[:, s % RING, :], hid[:, s % RING, :],
                                        hid_hi[:, s % RING, :].bitcast(F32), ALU.subtract).then_inc(hid_lo_pool, 1)

            run_blocks(pool, tick)

        @block.scalar
        def _(act):
            def x_high(k):
                act.wait_ge(xT_done, k + 1)
                nc.scalar.copy(x_hi[:, k, :], T_BANK[:]).then_inc(x_hi_ready, 1)

            def kq_high(k):
                act.wait_ge(kq_done, k + 1)
                if k >= 2:
                    act.wait_ge(sim_done, BPB * (k - 1))
                nc.scalar.activation(kq_hi[:, k % 2, :], K_BANK[0:CK, :], ACT.Identity,
                                     bias=bk[:]).then_inc(kq_hi_ready, 1)

            def u_copy(k):
                act.wait_ge(u_done, k + 1)
                nc.scalar.copy(u_sb[:, tiles(k), 0:C],
                               U_BANK[:, 0:TPB * C].rearrange("p (t c) -> p t c", c=C)).then_inc(u_copied, 1)

            def exponentials(b):
                act.wait_ge(max_ready, b + 1)
                if b >= 2:
                    act.wait_ge(probsT_done, b - 1)
                for i in range(2):
                    nc.scalar.activation(probs[:, b % 2, i, :], S_BANK[b % 2][:, N * i:N * (i + 1)], ACT.Exp,
                                         bias=neg_max[:, b, i:i + 1]).then_inc(probs_ready, 1)

            def probsT_copy(b):
                act.wait_ge(probsT_done, b + 1)
                if b >= 2:
                    act.wait_ge(attn_done, b - 1)
                nc.scalar.copy(probsT[:, b % 2, :, :], PT_BANK[b % 2][:]).then_inc(probsT_copied[1], 1)

            def t_high(k):
                act.wait_ge(tnT_done, k + 1)
                nc.scalar.copy(t_hi[:, cols(k)], T_BANK[:]).then_inc(hi_ready, 1)

            def split_high(q):
                r = q % 2
                act.wait_ge(raw_loaded[r], 16 * RAW_DMAS * (q // 2 + 1))
                nc.scalar.copy(w1_split[:, q, :], w1_raw[:, r, :]).then_inc(w_hi_made, 1)
                nc.scalar.copy(w3_split[:, q, :], w3_raw[:, r, :]).then_inc(w_hi_made, 1)
                nc.scalar.copy(w2_split[:, 2 * SLOTS * q:2 * SLOTS * (q + 1), 0, :],
                               w2_raw[:, r, :, :]).then_inc(w_hi_made, 1)

            x_high(0)
            act.wait_ge(consts_loaded, 16 * CONST_DMAS)
            kq_high(0)
            u_copy(0)
            split_high(0)

            for k in range(NBLK):
                exponentials(BPB * k)
                exponentials(BPB * k + 1)
                if k >= 1:
                    t_high(k - 1)
                probsT_copy(BPB * k + 1)
                if k + 1 < NBLK:
                    x_high(k + 1)
                if k + 1 < PAIRS:
                    split_high(k + 1)
                if k + 1 < NBLK:
                    kq_high(k + 1)
                    u_copy(k + 1)

            def tick(base, place, first, tail):
                s = place % STEPS
                n = step_no(base, place)
                if not tail:
                    act.wait_ge(h1_done, n + 1)
                    if not (first and place < 2):
                        act.wait_ge(hid_done, n - 1)
                    nc.scalar.activation(act_sb[:, s % 2, :], H1_BANK[s % 2][:], ACT.Silu).then_inc(silu_done, 1)
                if place >= 1 and place <= STEPS or not tail and not (first and place == 0):
                    r = (s - 1) % RING
                    act.wait_ge(hid_done, n)
                    if not (first and place < RING + 1):
                        act.wait_ge(hid_used, n - RING)
                    nc.scalar.copy(hid_hi[:, r, :], hid[:, r, :]).then_inc(hid_hi_made, 1)
                if first and place == ROUTE_AT - 2:
                    t_high(NBLK - 1)
                if first and place == ROUTE_AT:
                    act.wait_ge(shifted, 1)
                    nc.scalar.activation(expo[:], picked[:], ACT.Exp).then_inc(exponents, 1)
                if s == TRANSPOSE_T_AT + 1 and not tail:
                    act.wait_ge(tT_done, base + place // STEPS + 1)
                    nc.scalar.copy(tT[:, bass.ds((base + place // STEPS) * BLK, BLK)],
                                   bank[7][0:C, :]).then_inc(tT_copied, 1)
                if s in SPREAD_COPY_AT and not tail:
                    e = SPREAD_COPY_AT[s]
                    ee = base * E + E * (place // STEPS) + e
                    act.wait_ge(spread_done, ee + 1)
                    if not (first and e < 2):
                        act.wait_ge(y_gated, ee - 1)
                    nc.scalar.copy(gate_b[:, e % 2, :], bank[7][:]).then_inc(spread_copied, 1)

            run_blocks(act, tick)

        @block.vector
        def _(dve):
            steps = [0]

            def chain(ins):
                steps[0] += 1
                ins.then_inc(dve_step, 1)
                dve.wait_ge(dve_step, steps[0])

            def over_channels(v, n):
                return v.unsqueeze(2).to_broadcast([P, n, C])

            def statistics(norm, own, src):
                n = own.stop - own.start
                chain(nc.vector.tensor_reduce(mean[:, own], src, AX.X, ALU.add))
                chain(nc.vector.tensor_scalar(mean[:, own], mean[:, own], 1.0 / C, None, ALU.mult))
                chain(nc.vector.tensor_tensor(cent[:, own, :], src, over_channels(mean[:, own], n), ALU.subtract))
                chain(nc.vector.tensor_tensor(sq[:, own, :], cent[:, own, :], cent[:, own, :], ALU.mult))
                chain(nc.vector.tensor_reduce(ssq[:, own], sq[:, own, :], AX.X, ALU.add))
                nc.vector.tensor_scalar(var[:, norm, own], ssq[:, own], 1.0 / C, 1e-5 if norm else 1e-6,
                                        ALU.mult, ALU.add).then_inc(var_ready, 1)

            def normalise_x(n, own):
                dve.wait_ge(rstd_ready, n + 1)
                both = [P, own.stop - own.start, 2, C]
                nc.vector.tensor_tensor(xn[:, own, :, :], cent[:, own, :].unsqueeze(2).to_broadcast(both),
                                        rstd[:, 0, own].unsqueeze(2).unsqueeze(3).to_broadcast(both),
                                        ALU.mult).then_inc(xn_ready, 1)

            def t_statistics(k):
                dve.wait_ge(t_ready, TPB * (k + 1))
                if k == 0:
                    dve.wait_ge(xn_ready, 2)
                statistics(1, tiles(k), t_sb[:, tiles(k), :])

            def normalise_t(k):
                dve.wait_ge(rstd_ready, 3 + k)
                if k >= 2:
                    dve.wait_ge(tnT_done, k - 1)
                both = [P, TPB, 2, C]
                nc.vector.tensor_tensor(tn[:, k % 2, :, :, :], cent[:, tiles(k), :].unsqueeze(2).to_broadcast(both),
                                        rstd[:, 1, tiles(k)].unsqueeze(2).unsqueeze(3).to_broadcast(both),
                                        ALU.mult).then_inc(tn_ready, 1)

            def x_low(k):
                dve.wait_ge(x_hi_ready, k + 1)
                nc.vector.tensor_tensor(x_lo[:, k, :], T_BANK[:], x_hi[:, k, :].bitcast(F32),
                                        ALU.subtract).then_inc(x_lo_ready, 1)

            def kq_low(k):
                dve.wait_ge(kq_hi_ready, k + 1)
                if k >= 2:
                    dve.wait_ge(sim_done, BPB * (k - 1))
                nc.vector.scalar_tensor_tensor(out=kq_lo[:, k % 2, :], in0=K_BANK[0:CK, :], scalar=bk[:],
                                               in1=kq_hi[:, k % 2, :].bitcast(F32), op0=ALU.add,
                                               op1=ALU.subtract).then_inc(kq_lo_ready, 1)

            def row_max(b):
                dve.wait_ge(sim_done, b + 1)
                nc.vector.tensor_reduce(neg_max[:, b, :], S_BANK[b % 2][:].rearrange("p (i n) -> p i n", n=N),
                                        AX.X, ALU.max, negate=True).then_inc(max_ready, 1)

            def probsT_copy(b):
                dve.wait_ge(probsT_done, b + 1)
                if b >= 2:
                    dve.wait_ge(attn_done, b - 1)
                nc.vector.tensor_copy(probsT[:, b % 2, :, :], PT_BANK[b % 2][:].rearrange("p (j n) -> p j n", n=N)
                                      ).then_inc(probsT_copied[0], 1)

            def residual(b):
                at = (b % BPB) * 2 * (C + 1)
                o = O_BANK[:, at:at + 2 * (C + 1)].rearrange("p (i c) -> p i c", c=C + 1)
                dve.wait_ge(attn_done, BPB * (b // BPB + 1))
                if b == 0:
                    dve.wait_ge(bias_added, 1)
                nc.vector.reciprocal(inv_sum[:, b, :], o[:, :, C]).then_inc(sum_inverted, 1)
                dve.wait_ge(sum_inverted, b + 1)
                for i in range(2):
                    nc.vector.scalar_tensor_tensor(out=t_sb[:, 2 * b + i, :], in0=o[:, i, 0:C],
                                                   scalar=inv_sum[:, b, i:i + 1], in1=x_bias[:, 2 * b + i, :],
                                                   op0=ALU.mult, op1=ALU.add).then_inc(t_ready, 1)

            def t_low(k):
                dve.wait_ge(hi_ready, k + 1)
                nc.vector.tensor_tensor(t_lo[:, cols(k)], T_BANK[:], t_hi[:, cols(k)].bitcast(F32),
                                        ALU.subtract).then_inc(lo_ready, 1)

            def logits_copy(k):
                dve.wait_ge(logits_done, k + 1)
                nc.vector.tensor_copy(logits[:, tiles(k), :],
                                      K_BANK[:, 0:TPB * E].rearrange("p (t e) -> p t e", e=E)
                                      ).then_inc(logits_copied, 1)

            top, code, total, chosen, share, second = (small[:, i, :] for i in range(6))

            def per_e(v):
                return v.unsqueeze(2).to_broadcast([P, TILES, E])

            def largest(scores, value, mask):
                chain(nc.vector.tensor_tensor(mask, scores, per_e(value), ALU.is_equal))
                chain(nc.vector.tensor_tensor(mask, mask, order_val[:].unsqueeze(1).to_broadcast([P, TILES, E]),
                                              ALU.mult))
                chain(nc.vector.tensor_reduce(code, mask, AX.X, ALU.max))
                chain(nc.vector.tensor_tensor(mask, mask, per_e(code), ALU.is_equal))

            def route(part):
                if part == 0:
                    largest(logits[:], top, is_top[:, 0])
                if part == 1:
                    chain(nc.vector.scalar_tensor_tensor(out=rest[:], in0=is_top[:, 0], scalar=-3e38, in1=logits[:],
                                                         op0=ALU.mult, op1=ALU.add))
                    chain(nc.vector.tensor_reduce(second, rest[:], AX.X, ALU.max))
                if part == 2:
                    largest(rest[:], second, is_top[:, 1])
                if part == 3:
                    chain(nc.vector.tensor_tensor(is_top[:, 0], is_top[:, 0], is_top[:, 1], ALU.add))
                    dve.wait_ge(exponents, 1)
                    chain(nc.vector.tensor_tensor(picked[:], is_top[:, 0], expo[:], ALU.mult))
                if part == 4:
                    nc.vector.tensor_reduce(chosen, picked[:], AX.X, ALU.add).then_inc(dve_step, 1)
                    steps[0] += 1
                    chain(nc.vector.tensor_reduce(total, expo[:], AX.X, ALU.add))
                    chain(nc.vector.scalar_tensor_tensor(out=share, in0=total, scalar=1e-9, in1=chosen,
                                                         op0=ALU.mult, op1=ALU.add))
                    chain(nc.vector.reciprocal(share, share))
                if part == 5:
                    chain(nc.vector.tensor_tensor(picked[:], picked[:], per_e(share), ALU.mult))
                    chain(nc.vector.tensor_copy(gates[:, :, 0, :], picked[:]))
                    nc.vector.tensor_tensor(gates[:, :, 1, :], picked[:], gates[:, :, 0, :].bitcast(F32),
                                            ALU.subtract).then_inc(gates_ready, 1)
                    dve.wait_ge(gates_ready, 1)

            nc.vector.memset(ones_row[:], 1.0).then_inc(dve_consts, 1)
            nc.vector.memset(u_sb[:, :, C:C + 1], 1.0).then_inc(dve_consts, 1)
            first, others = tiles(0), slice(TPB, TILES)
            dve.wait_ge(x_loaded[0], 16)
            statistics(0, first, x_sb[:, first, :])
            dve.wait_ge(consts_loaded, 16 * CONST_DMAS)
            for whole, split in ((router_raw[:], router), (wk_raw[:], wk)):
                chain(nc.vector.tensor_copy(split[:], whole))
                nc.vector.tensor_tensor(split[C:P, :], whole[C:P, :], split[C:P, :].bitcast(F32),
                                        ALU.subtract).then_inc(dve_consts, 1)
            normalise_x(0, first)
            dve.wait_ge(wu_done, 1)
            chain(nc.vector.tensor_copy(wu[:], bank[0][:, 0:C]))
            nc.vector.tensor_tensor(wu[C:P, :], bank[0][C:P, 0:C], wu[C:P, :].bitcast(F32),
                                    ALU.subtract).then_inc(dve_consts, 1)
            dve.wait_ge(bias_done, 1)
            nc.vector.tensor_copy(bias[:], bank[1][:, 0:C]).then_inc(bias_copied, 1)
            x_low(0)
            for k in range(1, NBLK):
                dve.wait_ge(x_loaded[k], 16)
            statistics(0, others, x_sb[:, others, :])
            kq_low(0)
            row_max(0)
            normalise_x(1, others)
            row_max(1)
            for k in range(NBLK):
                if k >= 1:
                    t_low(k - 1)
                else:
                    dve.wait_ge(consts_made, 3)
                    nc.vector.tensor_tensor(pick_gate[:], ident[0:2 * E, 0:E].unsqueeze(2).to_broadcast([2 * E, E, P]),
                                            ident[0:2 * E, E:2 * E].unsqueeze(2).to_broadcast([2 * E, E, P]),
                                            ALU.add).then_inc(dve_consts, 1)
                    nc.vector.tensor_tensor(fold[:], ident[:, 0:C], ident[:, C:P], ALU.add).then_inc(dve_consts, 1)
                probsT_copy(BPB * k)
                if k + 1 < NBLK:
                    x_low(k + 1)
                if k >= 1:
                    logits_copy(k - 1)
                for b in range(BPB * k, BPB * (k + 1)):
                    residual(b)
                if k + 1 < NBLK:
                    kq_low(k + 1)
                t_statistics(k)
                if k + 1 < NBLK:
                    row_max(BPB * (k + 1))
                    normalise_t(k)
                    row_max(BPB * (k + 1) + 1)

            def last_block(place):
                if place == 0:
                    normalise_t(NBLK - 1)
                if place == ROUTE_AT - 2:
                    t_low(NBLK - 1)
                if place == ROUTE_AT - 1:
                    logits_copy(NBLK - 1)
                    dve.wait_ge(logits_copied, NBLK)
                    chain(nc.vector.tensor_reduce(top, logits[:], AX.X, ALU.max))
                    nc.vector.tensor_tensor(picked[:], logits[:], per_e(top), ALU.subtract).then_inc(shifted, 1)
                for part in {ROUTE_AT: (0, 1), ROUTE_AT + 1: (2,), ROUTE_AT + 2: (3, 4), ROUTE_AT + 3: (5,)}.get(place, ()):
                    route(part)

            def tick(base, place, first, tail):
                blk, s = divmod(place, STEPS)
                n = step_no(base, place)
                if s == STAGE_AT and not tail:
                    if not first:
                        dve.wait_ge(gateT_done, base + blk)
                    nc.vector.tensor_copy(gate_stage[:].rearrange("p t (h e) -> p t h e", e=E),
                                          gates[:, bass.ds((base + blk) * TPB, TPB), :, :].bitcast(F32)
                                          ).then_inc(stage_copied, 1)
                if not tail:
                    dve.wait_ge(silu_done, n + 1)
                    dve.wait_ge(h3_done, n + 1)
                    if not (first and place < RING):
                        dve.wait_ge(hid_hi_made, n - RING + 1)
                        lo_wait(dve, base, place - RING)
                    nc.vector.tensor_tensor(hid[:, s % RING, :], H3_BANK[s % 2][:], act_sb[:, s % 2, :],
                                            ALU.mult).then_inc(hid_done, 1)
                if first:
                    last_block(place)
                if s == STAGE_AT + 2 and not tail:
                    dve.wait_ge(gateT_done, base + blk + 1)
                    if not first:
                        dve.wait_ge(spread_done, (base + blk) * E)
                    nc.vector.tensor_copy(gateT[:], bank[6][0:2 * E, :]).then_inc(bank6_read, 1)
                if s == TRANSPOSE_T_AT - 2 and not tail:
                    if not first:
                        dve.wait_ge(tT_done, base + blk)
                    nc.vector.tensor_copy(t_stage[:], t_sb[:, bass.ds((base + blk) * TPB, TPB), :].unsqueeze(2)
                                          .to_broadcast([P, TPB, 2, C])).then_inc(t_staged, 1)
                s2 = (s - 2) % STEPS
                if s2 in DVE_LO and not (first and place < 2) and place - 2 < (STEPS if tail else 2 * STEPS):
                    dve.wait_ge(hid_hi_made, n - 1)
                    if not (first and place - 2 < RING):
                        dve.wait_ge(hid_used, n - 2 - RING + 1)
                    nc.vector.tensor_tensor(hid_lo[:, s2 % RING, :], hid[:, s2 % RING, :],
                                            hid_hi[:, s2 % RING, :].bitcast(F32), ALU.subtract
                                            ).then_inc(hid_lo_dve, 1)
                if s in GATE_AT:
                    e, late = GATE_AT[s]
                    of = blk - late
                    if of >= 0 and not (tail and of > 0):
                        ee = base * E + of * E + e
                        dve.wait_ge(hid_used, step_no(base, of * STEPS + LAST[e]) + 1)
                        dve.wait_ge(spread_copied, ee + 1)
                        if e == 0:
                            if not first:
                                dve.wait_ge(fold_done, base + of)
                            nc.vector.tensor_tensor(acc[:], Y_BANK[e % 2][:], gate_b[:, e % 2, :],
                                                    ALU.mult).then_inc(y_gated, 1)
                        else:
                            if e > 1:
                                dve.wait_ge(acc_added, (base + of) * (E - 1) + e - 1)
                            nc.vector.tensor_tensor(gated[:], Y_BANK[e % 2][:], gate_b[:, e % 2, :],
                                                    ALU.mult).then_inc(y_gated, 1)
                            dve.wait_ge(y_gated, ee + 1)
                            nc.vector.tensor_tensor(acc[:], acc[:], gated[:], ALU.add).then_inc(acc_added, 1)
                if s == RESULT_AT and not first and not (tail and blk == 0):
                    dve.wait_ge(fold_done, base + blk)
                    dve.wait_ge(tT_copied, base + blk)
                    res = tT[:, bass.ds((base + blk - 1) * BLK, BLK)]
                    nc.vector.tensor_tensor(res, bank[6][0:C, :], res, ALU.add).then_inc(bank6_read, 1)

            run_blocks(dve, tick)

        @block.tensor
        def _(pe):
            def transpose_x(k):
                pe.wait_ge(xn_ready, min(k, 1) + 1)
                if k >= 1:
                    pe.wait_ge(x_lo_ready, k)
                if k >= 2:
                    pe.wait_ge(lo_ready, k - 1)
                for t in range(TPB):
                    ins = nc.tensor.transpose(T_BANK[:, P * t:P * (t + 1)], xn[:, TPB * k + t, :, :], ident[:])
                ins.then_inc(xT_done, 1)

            def key_query(k):
                pe.wait_ge(x_hi_ready, k + 1)
                if k >= 1:
                    pe.wait_ge(kq_lo_ready, k)
                if k >= 2:
                    pe.wait_ge(logits_copied, k - 1)
                nc.tensor.matmul(K_BANK[0:CK, :], wk[:], x_hi[:, k, :], start=True, stop=False)
                pe.wait_ge(x_lo_ready, k + 1)
                nc.tensor.matmul(K_BANK[0:CK, :], wk[:], x_lo[:, k, :], start=False,
                                 stop=True).then_inc(kq_done, 1)

            def value_out(k):
                if k >= 1:
                    pe.wait_ge(u_copied, k)
                for t in range(TPB):
                    for part, ends in ((x_hi, (True, False)), (x_lo, (False, True))):
                        ins = nc.tensor.matmul(U_BANK[:, C * t:C * (t + 1)], part[:, k, P * t:P * (t + 1)],
                                               wu[:], start=ends[0], stop=ends[1])
                ins.then_inc(u_done, 1)

            def similarity(b):
                k, i0 = b // BPB, N * (b % BPB)
                pe.wait_ge(kq_hi_ready, k + 1)
                pe.wait_ge(kq_lo_ready, k + 1)
                if b >= 2:
                    pe.wait_ge(probs_ready, 2 * (b - 1))
                for i in range(2):
                    n = 0
                    for left in (kq_hi, kq_lo):
                        for right in (kq_hi, kq_lo):
                            ins = nc.tensor.matmul(S_BANK[b % 2][:, N * i:N * (i + 1)],
                                                   left[:, k % 2, i0 + P * i:i0 + P * (i + 1)],
                                                   right[:, k % 2, i0:i0 + N], start=(n == 0), stop=(n == 3))
                            n += 1
                ins.then_inc(sim_done, 1)

            def transpose_probs(b):
                pe.wait_ge(probs_ready, 2 * (b + 1))
                if b >= 2:
                    pe.wait_ge(probsT_copied[b % 2], b // 2)
                for i in range(2):
                    for j in range(2):
                        ins = nc.tensor.transpose(PT_BANK[b % 2][:, N * j + P * i:N * j + P * (i + 1)],
                                                  probs[:, b % 2, i, P * j:P * (j + 1)], ident[:])
                ins.then_inc(probsT_done, 1)

            def attend(b):
                at = (b % BPB) * 2 * (C + 1)
                pe.wait_ge(probsT_copied[b % 2], b // 2 + 1)
                pe.wait_ge(u_copied, b // BPB + 1)
                if b >= 2:
                    pe.wait_ge(t_ready, TPB * (b // BPB))
                for i in range(2):
                    for j in range(2):
                        ins = nc.tensor.matmul(O_BANK[:, at + (C + 1) * i:at + (C + 1) * (i + 1)],
                                               probsT[:, b % 2, j, P * i:P * (i + 1)], u_sb[:, 2 * b + j, :],
                                               start=(j == 0), stop=(j == 1))
                ins.then_inc(attn_done, 1)

            def transpose_t(k):
                pe.wait_ge(tn_ready, k + 1)
                pe.wait_ge(x_lo_ready, min(k + 2, NBLK))
                for t in range(TPB):
                    ins = nc.tensor.transpose(T_BANK[:, P * t:P * (t + 1)], tn[:, k % 2, t, :, :], ident[:])
                ins.then_inc(tnT_done, 1)

            def route(k):
                pe.wait_ge(lo_ready, k + 1)
                pe.wait_ge(kq_lo_ready, min(k + 2, NBLK))
                for t in range(TPB):
                    own = slice(BLK * k + P * t, BLK * k + P * (t + 1))
                    for part, ends in ((t_hi, (True, False)), (t_lo, (False, True))):
                        ins = nc.tensor.matmul(K_BANK[:, E * t:E * (t + 1)], part[:, own], router[:],
                                               start=ends[0], stop=ends[1])
                ins.then_inc(logits_done, 1)

            pe.wait_ge(consts_loaded, 16 * CONST_DMAS)
            pe.wait_ge(consts_made, 3)
            pe.wait_ge(dve_consts, 2)
            nc.tensor.matmul(bank[0][:, 0:C], wv[:], wo[:], start=True,
                             stop=True).then_inc(wu_done, 1)
            nc.tensor.matmul(bank[1][:, 0:C], bv[:].to_broadcast([CK, P]), wo[:], start=True, stop=False)
            nc.tensor.matmul(bank[1][:, 0:C], ones_row[:], bo[:], start=False, stop=True).then_inc(bias_done, 1)
            transpose_x(0)
            pe.wait_ge(dve_consts, 5)
            key_query(0)
            value_out(0)
            pe.wait_ge(bias_copied, 1)
            similarity(0)
            similarity(1)
            for k in range(NBLK):
                two = range(BPB * k, BPB * (k + 1))
                if k >= 1:
                    transpose_t(k - 1)
                for b in two:
                    transpose_probs(b)
                if k + 1 < NBLK:
                    transpose_x(k + 1)
                if k >= 1:
                    route(k - 1)
                for b in two:
                    attend(b)
                if k + 1 < NBLK:
                    key_query(k + 1)
                    value_out(k + 1)
                    similarity(BPB * (k + 1))
                    similarity(BPB * (k + 1) + 1)

            def up(base, place, first):
                blk, s = divmod(place, STEPS)
                n = step_no(base, place)
                q, j = divmod(s, CHUNKS)
                if place < STEPS and j == 0 and (first or base is NBLK - 1 or True):
                    pe.wait_ge(w_hi_made, 3 * (q + 1))
                    pe.wait_ge(w_lo_made, 3 * (q + 1))
                own = bass.ds((base + blk) * BLK, BLK)
                for split, banks, freed, done in ((w1_split, H1_BANK, silu_done, h1_done),
                                                  (w3_split, H3_BANK, hid_done, h3_done)):
                    w = split[:, q, P * j:P * (j + 1)]
                    if not (first and place < 2):
                        pe.wait_ge(freed, n - 1)
                    nc.tensor.matmul(banks[s % 2][:], w, t_hi[:, own], start=True, stop=False)
                    nc.tensor.matmul(banks[s % 2][:], w, t_lo[:, own], start=False, stop=True).then_inc(done, 1)

            def down(base, place, first):
                blk, s = divmod(place, STEPS)
                q, j = divmod(s, CHUNKS)
                pe.wait_ge(hid_hi_made, step_no(base, place) + 1)
                lo_wait(pe, base, place)
                slots = ([(0, j)] if j <= SEAM else []) + ([(1, j - SEAM)] if j >= SEAM else [])
                for side, slot in slots:
                    if slot == 0 and not (first and q == 0):
                        pe.wait_ge(y_gated, (base + blk) * E + 2 * q + side - 1)
                    w = w2_split[:, 2 * SLOTS * q + SLOTS * side + slot, :, :]
                    nc.tensor.matmul(Y_BANK[side][:], w, hid_hi[:, s % RING, :], start=(slot == 0), stop=False)
                    ins = nc.tensor.matmul(Y_BANK[side][:], w, hid_lo[:, s % RING, :], start=False,
                                           stop=(slot == SEAM))
                ins.then_inc(hid_used, 1)

            def tick(base, place, first, tail):
                blk, s = divmod(place, STEPS)
                if not tail:
                    up(base, place, first)
                if first and place == ROUTE_AT - 3:
                    transpose_t(NBLK - 1)
                if first and place == ROUTE_AT - 1:
                    route(NBLK - 1)
                if s == STAGE_AT + 1 and not tail:
                    pe.wait_ge(stage_copied, base + blk + 1)
                    if not first:
                        pe.wait_ge(bank6_read, (base + blk) * 2 - 1)
                    for t in range(TPB):
                        ins = nc.tensor.transpose(bank[6][0:2 * E, P * t:P * (t + 1)], gate_stage[:, t, :], ident[:])
                    ins.then_inc(gateT_done, 1)
                if s == TRANSPOSE_T_AT and not tail:
                    pe.wait_ge(t_staged, base + blk + 1)
                    pe.wait_ge(spread_copied, (base + blk) * E + 2)
                    for t in range(TPB):
                        ins = nc.tensor.transpose(bank[7][:, P * t:P * (t + 1)], t_stage[:, t, :, :], ident[:])
                    ins.then_inc(tT_done, 1)
                if place >= LAG and (not tail or place - LAG < STEPS):
                    down(base, place - LAG, first)
                if s in SPREAD_AT and not tail:
                    e = SPREAD_AT[s]
                    ee = base * E + blk * E + e
                    if e == 0:
                        pe.wait_ge(bank6_read, 1 if first else (base + blk) * 2)
                    if e == 2:
                        pe.wait_ge(tT_copied, base + blk + 1)
                    if not (first and e == 0):
                        pe.wait_ge(spread_copied, ee)
                    nc.tensor.matmul(bank[7][:], pick_gate[:, e, :], gateT[:], start=True,
                                     stop=True).then_inc(spread_done, 1)
                if s == FOLD_AT and not first and not (tail and blk == 0):
                    pe.wait_ge(acc_added, (base + blk) * (E - 1))
                    pe.wait_ge(bank6_read, (base + blk) * 2 - (1 if tail else 0))
                    nc.tensor.matmul(bank[6][0:C, :], fold[:], acc[:], start=True, stop=True).then_inc(fold_done, 1)

            pe.wait_ge(dve_consts, 7)
            run_blocks(pe, tick)


def kernel(**inputs):
    import numpy as np
    import concourse.bacc as bacc
    from concourse.bass_utils import run_bass_kernel_spmd

    a = {k: np.asarray(v) for k, v in inputs.items()}

    def experts(w):
        w = w.reshape(PAIRS, 2 * H, C).transpose(2, 0, 1)
        return np.concatenate([w, np.zeros((C, PAIRS, PW - 2 * H), w.dtype)], axis=2)

    w2 = np.zeros((PAIRS, 2, SLOTS * P, C), a["L0_ffn_w2"].dtype)
    rows = a["L0_ffn_w2"].transpose(0, 2, 1).reshape(PAIRS, 2, H, C)
    w2[:, 0, 0:H] = rows[:, 0]
    at = H - SEAM * P
    w2[:, 1, at:at + H] = rows[:, 1]
    arrays = {
        "x_tok": a["x"].reshape(B, C, N // P, P).transpose(3, 0, 2, 1).reshape(P, TILES, C),
        "wk_t": a["L0_conv_w_kq"].T,
        "b_kq": a["L0_conv_b_kq"][:, None],
        "w_v": a["L0_conv_w_v"],
        "b_v": a["L0_conv_b_v"][:, None],
        "wo_t": a["L0_conv_w_o"].T,
        "b_o": a["L0_conv_b_o"][None],
        "router_t": a["L0_ffn_router_w"].T,
        "w1_t": experts(a["L0_ffn_w1"]),
        "w3_t": experts(a["L0_ffn_w3"]),
        "w2_t": w2.reshape(PAIRS, 2 * SLOTS, P, C).transpose(2, 0, 1, 3),
    }
    arrays = {k: np.ascontiguousarray(v) for k, v in arrays.items()}
    nc = bacc.Bacc("TRN2", target_bir_lowering=False, num_devices=1)
    args = [nc.dram_tensor(k, v.shape, F32, kind="ExternalInput").ap() for k, v in arrays.items()]
    out = nc.dram_tensor("out", (B, C, N), F32, kind="ExternalOutput").ap()
    metaformer(nc, *args, out.rearrange("b c n -> c b n"))
    got = run_bass_kernel_spmd(nc, [arrays], core_ids=[0]).results[0]["out"]
    return got.reshape(B, C, 16, 16)
```

```python
from contextlib import ExitStack

import concourse.bass as bass
from concourse import mybir

F32 = mybir.dt.float32
F32R = mybir.dt.float32r
ALU = mybir.AluOpType
ACT = mybir.ActivationFunctionType
AX = mybir.AxisListType

B, C, N = 8, 64, 256
CK = 32
E, H = 8, 682
P = 128
TILES = B * N // P
BLK = 512
NBLK = B * N // BLK
TPB = BLK // P
BPB = BLK // N
PAIRS = E // 2
CHUNKS = -(-2 * H // P)
SEAM = H // P
SLOTS = SEAM + 1
PW = CHUNKS * P
STEPS = PAIRS * CHUNKS
LAG = 4
RING = 4
EPS = (1e-6, 1e-5)
ROT = 16
DVE_LO = (6, 11, 16, 22, 27, 33, 38, 43)


def metaformer(nc, x_tok, projections, value_output, b_o, w1_t, w3_t, w2_t, gates_dram, out):
    with ExitStack() as ctx:
        def sb(name, shape, dt=F32):
            return ctx.enter_context(nc.sbuf_tensor(name, shape, dt))

        def sem(name):
            return ctx.enter_context(nc.semaphore(name))

        bank = [ctx.enter_context(nc.psum_tensor(f"bank{i}", [P, BLK], F32)) for i in range(8)]

        ident = sb("ident", [P, P])
        order_val = sb("order_val", [P, E])
        neg_half = sb("neg_half", [P, TILES])
        ones_row = sb("ones_row", [1, P])
        w1_raw = sb("w1_raw", [P, 2, PW])
        w3_raw = sb("w3_raw", [P, 2, PW])
        w2_raw = sb("w2_raw", [P, 2, 2 * SLOTS, C])
        w1_split = sb("w1_split", [P, PAIRS, PW], F32R)
        w3_split = sb("w3_split", [P, PAIRS, PW], F32R)
        w2_split = sb("w2_split", [P, PAIRS * 2 * SLOTS, 2, C], F32R)
        proj = sb("proj", [P, CK + E + 1])
        wk = sb("wk", [P, P // CK, CK], F32R)
        vo = sb("vo", [CK, 3 * C + 1])
        bo = sb("bo", [1, C])
        wu = sb("wu", [P, C], F32R)
        router = sb("router", [P, E], F32R)
        x_sb = sb("x_sb", [P, TILES, C])
        x_bias = sb("x_bias", [P, TILES, C])
        t_sb = sb("t_sb", [P, TILES, C])
        tn = sb("tn", [P, 2, TPB, 2, C])
        parts = sb("parts", [P, 2, TILES, 6])
        moments = sb("moments", [P, 2, TILES, 2])
        variance = sb("variance", [P, 2, TILES])
        rstd = sb("rstd", [P, 2, TILES])
        t_hi = sb("t_hi", [P, NBLK * BLK], F32R)
        t_lo = sb("t_lo", [P, NBLK * BLK], F32R)
        tT = sb("tT", [C, NBLK * BLK])
        u_sb = sb("u_sb", [P, TILES, C + 1])
        neg_max = sb("neg_max", [P, B, 2])
        bias = sb("bias", [P, C])
        inv_sum = sb("inv_sum", [P, B, 2])
        logits = sb("logits", [P, TILES, E])
        probsT = sb("probsT", [P, 2, 2, N])
        small = sb("small", [P, 6, TILES])
        is_top = sb("is_top", [P, 2, TILES, E])
        rest = sb("rest", [P, TILES, E])
        expo = sb("expo", [P, TILES, E])
        picked = sb("picked", [P, TILES, E])
        t_stage = sb("t_stage", [P, TPB, 2, C])
        gates = sb("gates", [P, TILES * E])
        gatesT = sb("gatesT", [P, P])
        act_sb = sb("act_sb", [P, 2, BLK])
        hid = sb("hid", [P, RING, BLK])
        hid_hi = sb("hid_hi", [P, RING, BLK], F32R)
        hid_lo = sb("hid_lo", [P, RING, BLK], F32R)
        gate_b = sb("gate_b", [P, 2, BLK])
        gated = sb("gated", [P, BLK])
        acc = sb("acc", [P, BLK])
        half = sb("half", [C, BLK])
        x_hi = t_hi[:].rearrange("p (k n) -> p k n", n=BLK)
        x_lo = t_lo[:].rearrange("p (k n) -> p k n", n=BLK)
        probs = act_sb[:].rearrange("p r (i n) -> p r i n", n=N)
        kq_left, kq_right = hid_hi[:, 2:4, :], hid_lo[:, 2:4, :]
        xn = hid[:].rearrange("p r (t h c) -> p (r t) h c", h=2, c=C)

        wv, wo = vo[:, 0:2 * C], vo[:, 2 * C:3 * C]
        bk, bv = proj[:, CK + E:], vo[:, 3 * C:]

        x_loaded = [sem("x_loaded_first"), sem("x_loaded_rest")]
        consts_loaded = sem("consts_loaded")
        raw_loaded = [sem("raw_loaded0"), sem("raw_loaded1")]
        stored = sem("stored")
        consts_made = sem("consts_made")
        ident_zeroed = sem("ident_zeroed")
        dve_step = sem("dve_step")
        dve_consts = sem("dve_consts")
        moments_ready = sem("moments_ready")
        variance_ready = sem("variance_ready")
        rstd_ready = sem("rstd_ready")
        xn_ready = sem("xn_ready")
        xT_done, x_hi_ready, x_lo_ready = sem("xT_done"), sem("x_hi_ready"), sem("x_lo_ready")
        kq_done, kq_hi_ready, kq_lo_ready = sem("kq_done"), sem("kq_hi_ready"), sem("kq_lo_ready")
        kq_stacked = [sem("kq_stacked_act"), sem("kq_stacked_dve")]
        u_done, u_copied = sem("u_done"), sem("u_copied")
        wu_done, bias_done, bias_added = sem("wu_done"), sem("bias_done"), sem("bias_added")
        bias_copied = sem("bias_copied")
        sim_done = sem("sim_done")
        max_ready = sem("max_ready")
        probs_ready = sem("probs_ready")
        probsT_done = sem("probsT_done")
        probsT_copied = [sem("probsT_copied_dve"), sem("probsT_copied_act")]
        attn_done = sem("attn_done")
        sum_inverted = sem("sum_inverted")
        t_ready = sem("t_ready")
        tn_ready = sem("tn_ready")
        tnT_done = sem("tnT_done")
        hi_ready, lo_ready = sem("t_hi_ready"), sem("t_lo_ready")
        t_staged = sem("t_staged")
        tT_done, tT_copied = sem("tT_done"), sem("tT_copied")
        logits_done, logits_copied = sem("logits_done"), sem("logits_copied")
        shifted, exponents = sem("shifted"), sem("exponents")
        gates_ready = sem("gates_ready")
        w_hi_made, w_lo_made = sem("w_hi_made"), sem("w_lo_made")
        h1_done, h3_done = sem("h1_done"), sem("h3_done")
        silu_done = sem("silu_done")
        hid_done = sem("hid_done")
        hid_hi_made = sem("hid_hi_made")
        hid_lo_pool, hid_lo_dve = sem("hid_lo_pool"), sem("hid_lo_dve")
        hid_used = sem("hid_used")
        gates_turned, gatesT_ready = sem("gates_turned"), sem("gatesT_ready")
        gates_stored = sem("gates_stored")
        gate_loaded = [sem("gate_loaded0"), sem("gate_loaded1")]
        y_gated = sem("y_gated")
        acc_added = sem("acc_added")
        half_moved, half_added = sem("half_moved"), sem("half_added")
        result_ready = sem("result_ready")

        S_BANK, PT_BANK, O_BANK, U_BANK = bank[0:2], bank[2:4], bank[4], bank[5]
        T_BANK, K_BANK = bank[6], bank[7]
        H1_BANK, H3_BANK, Y_BANK = bank[0:2], bank[2:4], bank[4:6]
        CONST_DMAS = 3
        RAW_DMAS = 5

        def tiles(k):
            return slice(TPB * k, TPB * (k + 1))

        def cols(k):
            return slice(BLK * k, BLK * (k + 1))

        def step_no(base, place):
            return base * STEPS + place

        def lo_wait(eng, base, place):
            blk, s = divmod(place, STEPS)
            n_dve = sum(d < s for d in DVE_LO)
            if s in DVE_LO:
                eng.wait_ge(hid_lo_dve, base * len(DVE_LO) + blk * len(DVE_LO) + n_dve + 1)
            else:
                n_pool = STEPS - len(DVE_LO)
                eng.wait_ge(hid_lo_pool, base * n_pool + blk * n_pool + s - n_dve + 1)

        FIRST = [CHUNKS * (e // 2) + SEAM * (e % 2) for e in range(E)]
        LAST = [f + SEAM for f in FIRST]
        ROUTE_AT = 4
        TURN_AT = ROUTE_AT + 5
        TRANSPOSE_T_AT = 15
        GATE_AT = {(l + LAG + 1 + (e == 1)) % STEPS: (e, (l + LAG + 1) // STEPS)
                   for e, l in enumerate(LAST) if e}
        GATE_AT[13] = (0, 0)
        FOLD_AT, RESULT_AT = 11, 12
        TAIL = RESULT_AT + 1

        def run_blocks(eng, tick):
            for place in range(ROT):
                tick(0, place, first=True, tail=False)
            with eng.Fori(0, NBLK - 1) as blk:
                for place in range(ROT, STEPS + ROT):
                    tick(blk, place, first=False, tail=False)
            for place in range(ROT, STEPS + TAIL):
                tick(NBLK - 1, place, first=False, tail=place >= STEPS)

        block = ctx.enter_context(nc.Block())

        @block.sync
        def _(sp):
            own = (tiles(0), slice(TPB, TILES))
            sp.dma_start(x_sb[:, own[0], :], x_tok[:, own[0], :]).then_inc(x_loaded[0], 16)
            sp.dma_start(proj[:], projections).then_inc(consts_loaded, 16)
            sp.dma_start(vo[:], value_output).then_inc(consts_loaded, 16)
            sp.dma_start(bo[:], b_o).then_inc(consts_loaded, 16)
            sp.dma_start(x_sb[:, own[1], :], x_tok[:, own[1], :]).then_inc(x_loaded[1], 16)
            for q in range(PAIRS):
                r = q % 2
                if q >= 2:
                    sp.wait_ge(w_lo_made, 3 * (q - 1))
                for raw, src in ((w1_raw, w1_t), (w3_raw, w3_t)):
                    for rows in (slice(0, C), slice(C, P)):
                        sp.dma_start(raw[rows, r, :], src[:, q, :]).then_inc(raw_loaded[r], 16)
                sp.dma_start(w2_raw[:, r, :, :], w2_t[:, q, :, :]).then_inc(raw_loaded[r], 16)
            sp.wait_ge(gatesT_ready, 1)
            sp.dma_start(gates_dram, gatesT[:]).then_inc(gates_stored, 16)
            sp.wait_ge(gates_stored, 16)
            by_expert = gates_dram.rearrange("(t e) n -> e t n", e=E)

            def load_gate(blk, e):
                sp.dma_start(gate_b[:, e % 2, :].rearrange("p (t n) -> p t n", n=P),
                             by_expert[e, bass.ds(blk * TPB, TPB), :].partition_broadcast(P)
                             ).then_inc(gate_loaded[e % 2], 16)

            for e in range(E):
                if e >= 2:
                    sp.wait_ge(y_gated, e - 1)
                load_gate(0, e)
            with sp.Fori(0, NBLK - 1) as blk:
                for e in range(E):
                    sp.wait_ge(y_gated, (blk + 1) * E + e - 1)
                    load_gate(blk + 1, e)
                    if e == 1:
                        sp.wait_ge(result_ready, blk + 1)
                        sp.dma_start(out[:, bass.ds(blk * BPB, BPB), :],
                                     tT[:, bass.ds(blk * BLK, BLK)].rearrange("c (b n) -> c b n", n=N)
                                     ).then_inc(stored, 16)
            sp.wait_ge(result_ready, NBLK)
            sp.dma_start(out[:, BPB * (NBLK - 1):, :],
                         tT[:, cols(NBLK - 1)].rearrange("c (b n) -> c b n", n=N)).then_inc(stored, 16)
            sp.wait_ge(stored, 16 * NBLK)

        @block.gpsimd
        def _(pool):
            nc.gpsimd.memset(ident[:], 0.0).then_inc(ident_zeroed, 1)
            nc.gpsimd.memset(neg_half[:], -0.5).then_inc(consts_made, 1)
            pool.wait_ge(ident_zeroed, 1)
            nc.gpsimd.affine_select(out=ident[:], in_=ident[:], compare_op=ALU.not_equal, fill=1.0, base=0,
                                    pattern=[[-1, P]], channel_multiplier=1).then_inc(consts_made, 1)
            nc.gpsimd.iota(order_val[:], pattern=[[-1, E]], base=E, channel_multiplier=0,
                           allow_small_or_imprecise_dtypes=True).then_inc(consts_made, 1)

            def inverse_deviation(norm, k):
                pool.wait_ge(moments_ready, NBLK * norm + k + 1)
                nc.gpsimd.tensor_scalar(variance[:, norm, tiles(k)], moments[:, norm, tiles(k), 1], EPS[norm], None,
                                        ALU.add).then_inc(variance_ready, 1)
                pool.wait_ge(variance_ready, NBLK * norm + k + 1)
                nc.gpsimd.tensor_tensor(rstd[:, norm, tiles(k)], variance[:, norm, tiles(k)], neg_half[:, tiles(k)],
                                        ALU.pow).then_inc(rstd_ready, 1)

            def split_low_w1(q):
                pool.wait_ge(raw_loaded[q % 2], 16 * RAW_DMAS * (q // 2 + 1))
                if q >= 1:
                    pool.wait_ge(w_lo_made, 3 * q)
                pool.wait_ge(w_hi_made, 3 * q + 1)
                lo = w1_split[C:P, q, :]
                nc.gpsimd.tensor_tensor(lo, w1_raw[C:P, q % 2, :], lo.bitcast(F32), ALU.subtract).then_inc(w_lo_made, 1)

            def split_low_rest(q, before):
                pool.wait_ge(rstd_ready, before)
                pool.wait_ge(w_hi_made, 3 * q + 2)
                lo = w3_split[C:P, q, :]
                nc.gpsimd.tensor_tensor(lo, w3_raw[C:P, q % 2, :], lo.bitcast(F32), ALU.subtract).then_inc(w_lo_made, 1)
                pool.wait_ge(w_hi_made, 3 * q + 3)
                pool.wait_ge(w_lo_made, 3 * q + 2)
                part = slice(2 * SLOTS * q, 2 * SLOTS * (q + 1))
                nc.gpsimd.tensor_tensor(w2_split[:, part, 1, :], w2_raw[:, q % 2, :, :],
                                        w2_split[:, part, 0, :].bitcast(F32), ALU.subtract).then_inc(w_lo_made, 1)

            inverse_deviation(0, 0)
            inverse_deviation(0, 1)
            pool.wait_ge(bias_copied, 1)
            nc.gpsimd.tensor_tensor(x_bias[:], x_sb[:], bias[:].unsqueeze(1).to_broadcast([P, TILES, C]),
                                    ALU.add).then_inc(bias_added, 1)
            pool.wait_ge(bias_added, 1)
            split_low_w1(0)
            pool.wait_ge(w_lo_made, 1)
            inverse_deviation(0, 2)
            inverse_deviation(0, 3)
            split_low_rest(0, NBLK)
            for q in range(1, PAIRS):
                if q + 1 == PAIRS:
                    pool.wait_ge(w_lo_made, 3 * q)
                    inverse_deviation(1, q - 1)
                    pool.wait_ge(rstd_ready, NBLK + q)
                split_low_w1(q)
                pool.wait_ge(w_lo_made, 3 * q + 1)
                inverse_deviation(1, q if q + 1 == PAIRS else q - 1)
                split_low_rest(q, NBLK + q + (q + 1 == PAIRS))

            def tick(base, place, first, tail):
                s = place % STEPS
                if s in DVE_LO or tail:
                    return
                n = step_no(base, place)
                pool.wait_ge(hid_hi_made, n + 1)
                if not (first and place < RING):
                    pool.wait_ge(hid_used, n - RING + 1)
                nc.gpsimd.tensor_tensor(hid_lo[:, s % RING, :], hid[:, s % RING, :],
                                        hid_hi[:, s % RING, :].bitcast(F32), ALU.subtract).then_inc(hid_lo_pool, 1)

            run_blocks(pool, tick)

        @block.scalar
        def _(act):
            def x_high(k):
                act.wait_ge(xT_done, k + 1)
                nc.scalar.copy(x_hi[:, k, :], T_BANK[:]).then_inc(x_hi_ready, 1)

            def kq_high(k):
                act.wait_ge(kq_done, k + 1)
                if k >= 2:
                    act.wait_ge(sim_done, BPB * (k - 1))
                nc.scalar.activation(kq_left[:, k % 2, :], K_BANK[:], ACT.Identity, bias=bk).then_inc(kq_hi_ready, 1)

            def kq_stack(k):
                act.wait_ge(kq_hi_ready, k + 1)
                for rows in (slice(0, CK), slice(2 * CK, 3 * CK)):
                    nc.scalar.copy(kq_right[rows, k % 2, :], kq_left[0:CK, k % 2, :]).then_inc(kq_stacked[0], 1)

            def u_copy(k):
                act.wait_ge(u_done, k + 1)
                nc.scalar.copy(u_sb[:, tiles(k), 0:C],
                               U_BANK[:, 0:TPB * C].rearrange("p (t c) -> p t c", c=C)).then_inc(u_copied, 1)

            def exponentials(b):
                act.wait_ge(max_ready, b + 1)
                if b >= 2:
                    act.wait_ge(probsT_done, b - 1)
                for i in range(2):
                    nc.scalar.activation(probs[:, b % 2, i, :], S_BANK[b % 2][:, N * i:N * (i + 1)], ACT.Exp,
                                         bias=neg_max[:, b, i:i + 1]).then_inc(probs_ready, 1)

            def probsT_copy(b):
                act.wait_ge(probsT_done, b + 1)
                if b >= 2:
                    act.wait_ge(attn_done, b - 1)
                nc.scalar.copy(probsT[:, b % 2, :, :], PT_BANK[b % 2][:]).then_inc(probsT_copied[1], 1)

            def t_high(k):
                act.wait_ge(tnT_done, k + 1)
                nc.scalar.copy(t_hi[:, cols(k)], T_BANK[:]).then_inc(hi_ready, 1)

            def split_high_w1(q):
                act.wait_ge(raw_loaded[q % 2], 16 * RAW_DMAS * (q // 2 + 1))
                nc.scalar.copy(w1_split[:, q, :], w1_raw[:, q % 2, :]).then_inc(w_hi_made, 1)

            def split_high_rest(q):
                nc.scalar.copy(w3_split[:, q, :], w3_raw[:, q % 2, :]).then_inc(w_hi_made, 1)
                nc.scalar.copy(w2_split[:, 2 * SLOTS * q:2 * SLOTS * (q + 1), 0, :],
                               w2_raw[:, q % 2, :, :]).then_inc(w_hi_made, 1)

            x_high(0)
            act.wait_ge(consts_loaded, 16 * CONST_DMAS)
            kq_high(0)
            u_copy(0)
            kq_stack(0)
            split_high_w1(0)
            exponentials(0)
            exponentials(1)
            x_high(1)
            probsT_copy(1)
            kq_high(1)
            u_copy(1)
            kq_stack(1)
            split_high_rest(0)
            for k in range(NBLK):
                if k >= 1:
                    probsT_copy(BPB * k + 1)
                if k + 1 == NBLK:
                    split_high_rest(k)
                else:
                    exponentials(BPB * (k + 1))
                    exponentials(BPB * (k + 1) + 1)
                if k + 2 < NBLK:
                    x_high(k + 2)
                if k + 2 < NBLK:
                    split_high_w1(k + 1)
                    kq_high(k + 2)
                    u_copy(k + 2)
                    kq_stack(k + 2)
                if k >= 1:
                    t_high(k - 1)
                if k + 2 < NBLK:
                    split_high_rest(k + 1)
                elif k + 2 == NBLK:
                    split_high_w1(k + 1)

            def tick(base, place, first, tail):
                s = place % STEPS
                n = step_no(base, place)
                if not tail:
                    act.wait_ge(h1_done, n + 1)
                    if not (first and place < 2):
                        act.wait_ge(hid_done, n - 1)
                    nc.scalar.activation(act_sb[:, s % 2, :], H1_BANK[s % 2][:], ACT.Silu).then_inc(silu_done, 1)
                if place >= 1 and place <= STEPS or not tail and not (first and place == 0):
                    r = (s - 1) % RING
                    act.wait_ge(hid_done, n)
                    if not (first and place < RING + 1):
                        act.wait_ge(hid_used, n - RING)
                    nc.scalar.copy(hid_hi[:, r, :], hid[:, r, :]).then_inc(hid_hi_made, 1)
                if first and place == ROUTE_AT - 2:
                    t_high(NBLK - 1)
                if first and place == ROUTE_AT:
                    act.wait_ge(shifted, 1)
                    nc.scalar.activation(expo[:], picked[:], ACT.Exp).then_inc(exponents, 1)
                if s == TRANSPOSE_T_AT + 1 and not tail:
                    act.wait_ge(tT_done, base + place // STEPS + 1)
                    nc.scalar.copy(tT[:, bass.ds((base + place // STEPS) * BLK, BLK)],
                                   bank[7][0:C, :]).then_inc(tT_copied, 1)
                if s == FOLD_AT and not first and not (tail and place < STEPS):
                    act.wait_ge(acc_added, (base + place // STEPS) * (E - 1))
                    nc.scalar.copy(half[:], acc[C:P, :]).then_inc(half_moved, 1)

            run_blocks(act, tick)

        @block.vector
        def _(dve):
            steps = [0]

            def chain(ins):
                steps[0] += 1
                ins.then_inc(dve_step, 1)
                dve.wait_ge(dve_step, steps[0])

            def statistics(norm, k, src):
                for t in range(TPB * k, TPB * (k + 1)):
                    ins = nc.vector.bn_stats(parts[:, norm, t, :], src[:, t, :])
                chain(ins)
                for t in range(TPB * k, TPB * (k + 1)):
                    ins = nc.vector.bn_aggr(moments[:, norm, t, :], parts[:, norm, t, :])
                ins.then_inc(moments_ready, 1)

            def normalise(norm, k, src, dst, done):
                dve.wait_ge(rstd_ready, NBLK * norm + k + 1)
                for t in range(TPB):
                    tile = TPB * k + t
                    ins = nc.vector.tensor_scalar(dst[:, t, :, :], src[:, tile:tile + 1, :].to_broadcast([P, 2, C]),
                                                  moments[:, norm, tile, 0:1], rstd[:, norm, tile:tile + 1],
                                                  ALU.subtract, ALU.mult)
                ins.then_inc(done, 1)

            def normalise_x(k):
                normalise(0, k, x_sb, xn[:, tiles(k), :, :], xn_ready)

            def t_statistics(k):
                dve.wait_ge(t_ready, TPB * (k + 1))
                statistics(1, k, t_sb)

            def normalise_t(k):
                if k >= 2:
                    dve.wait_ge(tnT_done, k - 1)
                normalise(1, k, t_sb, tn[:, k % 2, :, :, :], tn_ready)

            def x_low(k):
                dve.wait_ge(x_hi_ready, k + 1)
                nc.vector.tensor_tensor(x_lo[:, k, :], T_BANK[:], x_hi[:, k, :].bitcast(F32),
                                        ALU.subtract).then_inc(x_lo_ready, 1)

            def kq_low(k):
                dve.wait_ge(kq_hi_ready, k + 1)
                if k >= 2:
                    dve.wait_ge(sim_done, BPB * (k - 1))
                low = kq_left[2 * CK:P, k % 2, :]
                nc.vector.scalar_tensor_tensor(out=low, in0=K_BANK[2 * CK:P, :], scalar=bk[2 * CK:P],
                                               in1=low.bitcast(F32), op0=ALU.add,
                                               op1=ALU.subtract).then_inc(kq_lo_ready, 1)
                dve.wait_ge(kq_lo_ready, k + 1)
                for rows in (slice(CK, 2 * CK), slice(3 * CK, P)):
                    nc.vector.tensor_copy(kq_right[rows, k % 2, :], kq_left[2 * CK:3 * CK, k % 2, :]
                                          ).then_inc(kq_stacked[1], 1)

            def row_max(b):
                dve.wait_ge(sim_done, b + 1)
                nc.vector.tensor_reduce(neg_max[:, b, :], S_BANK[b % 2][:].rearrange("p (i n) -> p i n", n=N),
                                        AX.X, ALU.max, negate=True).then_inc(max_ready, 1)

            def probsT_copy(b):
                dve.wait_ge(probsT_done, b + 1)
                if b >= 2:
                    dve.wait_ge(attn_done, b - 1)
                nc.vector.tensor_copy(probsT[:, b % 2, :, :], PT_BANK[b % 2][:].rearrange("p (j n) -> p j n", n=N)
                                      ).then_inc(probsT_copied[0], 1)

            def residual(b):
                at = (b % BPB) * 2 * (C + 1)
                o = O_BANK[:, at:at + 2 * (C + 1)].rearrange("p (i c) -> p i c", c=C + 1)
                dve.wait_ge(attn_done, BPB * (b // BPB + 1))
                if b == 0:
                    dve.wait_ge(bias_added, 1)
                nc.vector.reciprocal(inv_sum[:, b, :], o[:, :, C]).then_inc(sum_inverted, 1)
                dve.wait_ge(sum_inverted, b + 1)
                for i in range(2):
                    nc.vector.scalar_tensor_tensor(out=t_sb[:, 2 * b + i, :], in0=o[:, i, 0:C],
                                                   scalar=inv_sum[:, b, i:i + 1], in1=x_bias[:, 2 * b + i, :],
                                                   op0=ALU.mult, op1=ALU.add).then_inc(t_ready, 1)

            def t_low(k):
                dve.wait_ge(hi_ready, k + 1)
                nc.vector.tensor_tensor(t_lo[:, cols(k)], T_BANK[:], t_hi[:, cols(k)].bitcast(F32),
                                        ALU.subtract).then_inc(lo_ready, 1)

            def logits_copy(k):
                dve.wait_ge(logits_done, k + 1)
                nc.vector.tensor_copy(logits[:, tiles(k), :],
                                      K_BANK[:, 0:TPB * E].rearrange("p (t e) -> p t e", e=E)
                                      ).then_inc(logits_copied, 1)

            top, code, total, chosen, share, second = (small[:, i, :] for i in range(6))

            def per_e(v):
                return v.unsqueeze(2).to_broadcast([P, TILES, E])

            def largest(scores, value, mask):
                chain(nc.vector.tensor_tensor(mask, scores, per_e(value), ALU.is_equal))
                chain(nc.vector.tensor_tensor(mask, mask, order_val[:].unsqueeze(1).to_broadcast([P, TILES, E]),
                                              ALU.mult))
                chain(nc.vector.tensor_reduce(code, mask, AX.X, ALU.max))
                chain(nc.vector.tensor_tensor(mask, mask, per_e(code), ALU.is_equal))

            def route(part):
                if part == 0:
                    largest(logits[:], top, is_top[:, 0])
                if part == 1:
                    chain(nc.vector.scalar_tensor_tensor(out=rest[:], in0=is_top[:, 0], scalar=-3e38, in1=logits[:],
                                                         op0=ALU.mult, op1=ALU.add))
                    chain(nc.vector.tensor_reduce(second, rest[:], AX.X, ALU.max))
                if part == 2:
                    largest(rest[:], second, is_top[:, 1])
                if part == 3:
                    chain(nc.vector.tensor_tensor(is_top[:, 0], is_top[:, 0], is_top[:, 1], ALU.add))
                    dve.wait_ge(exponents, 1)
                    chain(nc.vector.tensor_tensor(picked[:], is_top[:, 0], expo[:], ALU.mult))
                if part == 4:
                    nc.vector.tensor_reduce(chosen, picked[:], AX.X, ALU.add).then_inc(dve_step, 1)
                    steps[0] += 1
                    chain(nc.vector.tensor_reduce(total, expo[:], AX.X, ALU.add))
                    chain(nc.vector.scalar_tensor_tensor(out=share, in0=total, scalar=1e-9, in1=chosen,
                                                         op0=ALU.mult, op1=ALU.add))
                    chain(nc.vector.reciprocal(share, share))
                if part == 5:
                    nc.vector.tensor_tensor(gates[:].rearrange("p (t e) -> p t e", e=E), picked[:], per_e(share),
                                            ALU.mult).then_inc(gates_ready, 1)

            nc.vector.memset(ones_row[:], 1.0).then_inc(dve_consts, 1)
            nc.vector.memset(u_sb[:, :, C:C + 1], 1.0).then_inc(dve_consts, 1)
            dve.wait_ge(x_loaded[0], 16)
            statistics(0, 0, x_sb)
            dve.wait_ge(consts_loaded, 16 * CONST_DMAS)
            for whole, split in ((proj[:, 0:CK].unsqueeze(1).to_broadcast([P, P // CK, CK]), wk),
                                 (proj[:, CK:CK + E], router)):
                chain(nc.vector.tensor_copy(split[:], whole))
                nc.vector.tensor_tensor(split[C:P], whole[C:P], split[C:P].bitcast(F32),
                                        ALU.subtract).then_inc(dve_consts, 1)
            normalise_x(0)
            dve.wait_ge(wu_done, 1)
            chain(nc.vector.tensor_copy(wu[:], bank[0][:, 0:C]))
            nc.vector.tensor_tensor(wu[C:P, :], bank[0][C:P, 0:C], wu[C:P, :].bitcast(F32),
                                    ALU.subtract).then_inc(dve_consts, 1)
            dve.wait_ge(bias_done, 1)
            nc.vector.tensor_copy(bias[:], bank[1][:, 0:C]).then_inc(bias_copied, 1)
            x_low(0)
            dve.wait_ge(x_loaded[1], 16)
            statistics(0, 1, x_sb)
            kq_low(0)
            normalise_x(1)
            row_max(0)
            row_max(1)
            x_low(1)
            probsT_copy(0)
            statistics(0, 2, x_sb)
            kq_low(1)
            statistics(0, 3, x_sb)
            for k in range(NBLK):
                if k >= 1:
                    probsT_copy(BPB * k)
                if k + 1 < NBLK:
                    row_max(BPB * (k + 1))
                    row_max(BPB * (k + 1) + 1)
                if k == 0:
                    normalise_x(2)
                if k >= 2:
                    logits_copy(k - 2)
                if k >= 1:
                    normalise_t(k - 1)
                if k + 2 < NBLK:
                    x_low(k + 2)
                residual(BPB * k)
                residual(BPB * k + 1)
                t_statistics(k)
                if k + 2 < NBLK:
                    kq_low(k + 2)
                if k + 3 < NBLK:
                    normalise_x(k + 3)
                if k >= 1:
                    t_low(k - 1)

            def last_block(place):
                if place == 0:
                    normalise_t(NBLK - 1)
                if place == ROUTE_AT - 2:
                    logits_copy(NBLK - 2)
                if place == ROUTE_AT - 2:
                    t_low(NBLK - 1)
                if place == ROUTE_AT - 1:
                    logits_copy(NBLK - 1)
                    dve.wait_ge(logits_copied, NBLK)
                    chain(nc.vector.tensor_reduce(top, logits[:], AX.X, ALU.max))
                    nc.vector.tensor_tensor(picked[:], logits[:], per_e(top), ALU.subtract).then_inc(shifted, 1)
                for part in {ROUTE_AT: (0, 1), ROUTE_AT + 1: (2,), ROUTE_AT + 2: (3, 4),
                             ROUTE_AT + 3: (5,)}.get(place, ()):
                    route(part)

            def tick(base, place, first, tail):
                blk, s = divmod(place, STEPS)
                n = step_no(base, place)
                if not tail:
                    dve.wait_ge(silu_done, n + 1)
                    dve.wait_ge(h3_done, n + 1)
                    if not (first and place < RING):
                        dve.wait_ge(hid_hi_made, n - RING + 1)
                        lo_wait(dve, base, place - RING)
                    nc.vector.tensor_tensor(hid[:, s % RING, :], H3_BANK[s % 2][:], act_sb[:, s % 2, :],
                                            ALU.mult).then_inc(hid_done, 1)
                if first:
                    last_block(place)
                if first and place == TURN_AT + 1:
                    dve.wait_ge(gates_turned, 1)
                    nc.vector.tensor_copy(gatesT[:], bank[6][:, 0:P]).then_inc(gatesT_ready, 1)
                if s == TRANSPOSE_T_AT - 2 and not tail:
                    if not first:
                        dve.wait_ge(tT_done, base + blk)
                    nc.vector.tensor_copy(t_stage[:], t_sb[:, bass.ds((base + blk) * TPB, TPB), :].unsqueeze(2)
                                          .to_broadcast([P, TPB, 2, C])).then_inc(t_staged, 1)
                s2 = (s - 2) % STEPS
                if s2 in DVE_LO and not (first and place < 2) and place - 2 < (STEPS if tail else 2 * STEPS):
                    dve.wait_ge(hid_hi_made, n - 1)
                    if not (first and place - 2 < RING):
                        dve.wait_ge(hid_used, n - 2 - RING + 1)
                    nc.vector.tensor_tensor(hid_lo[:, s2 % RING, :], hid[:, s2 % RING, :],
                                            hid_hi[:, s2 % RING, :].bitcast(F32), ALU.subtract
                                            ).then_inc(hid_lo_dve, 1)
                if s in GATE_AT:
                    e, late = GATE_AT[s]
                    of = blk - late
                    if of >= 0 and not (tail and of > 0):
                        ee = base * E + of * E + e
                        dve.wait_ge(hid_used, step_no(base, of * STEPS + LAST[e]) + 1)
                        dve.wait_ge(gate_loaded[e % 2], 16 * ((base + of) * (E // 2) + e // 2 + 1))
                        if e == 0:
                            if not first:
                                dve.wait_ge(result_ready, base + of)
                            nc.vector.tensor_tensor(acc[:], Y_BANK[e % 2][:], gate_b[:, e % 2, :],
                                                    ALU.mult).then_inc(y_gated, 1)
                        else:
                            if e > 1:
                                dve.wait_ge(acc_added, (base + of) * (E - 1) + e - 1)
                            nc.vector.tensor_tensor(gated[:], Y_BANK[e % 2][:], gate_b[:, e % 2, :],
                                                    ALU.mult).then_inc(y_gated, 1)
                            dve.wait_ge(y_gated, ee + 1)
                            nc.vector.tensor_tensor(acc[:], acc[:], gated[:], ALU.add).then_inc(acc_added, 1)
                if s in (FOLD_AT, RESULT_AT) and not first and not (tail and blk == 0):
                    res = tT[:, bass.ds((base + blk - 1) * BLK, BLK)]
                    if s == FOLD_AT:
                        dve.wait_ge(tT_copied, base + blk)
                        dve.wait_ge(acc_added, (base + blk) * (E - 1))
                        nc.vector.tensor_tensor(res, acc[0:C, :], res, ALU.add).then_inc(half_added, 1)
                    else:
                        dve.wait_ge(half_added, base + blk)
                        dve.wait_ge(half_moved, base + blk)
                        nc.vector.tensor_tensor(res, half[:], res, ALU.add).then_inc(result_ready, 1)

            run_blocks(dve, tick)

        @block.tensor
        def _(pe):
            def transpose_x(k):
                pe.wait_ge(xn_ready, k + 1)
                if k >= 1:
                    pe.wait_ge(x_lo_ready, k)
                for t in range(TPB):
                    ins = nc.tensor.transpose(T_BANK[:, P * t:P * (t + 1)], xn[:, TPB * k + t, :, :], ident[:])
                ins.then_inc(xT_done, 1)

            def key_query(k):
                pe.wait_ge(x_hi_ready, k + 1)
                if k >= 1:
                    pe.wait_ge(kq_lo_ready, k)
                nc.tensor.matmul(K_BANK[:], wk[:], x_hi[:, k, :], start=True, stop=False)
                pe.wait_ge(x_lo_ready, k + 1)
                nc.tensor.matmul(K_BANK[:], wk[:], x_lo[:, k, :], start=False, stop=True).then_inc(kq_done, 1)

            def value_out(k):
                if k >= 1:
                    pe.wait_ge(u_copied, k)
                for t in range(TPB):
                    for part, ends in ((x_hi, (True, False)), (x_lo, (False, True))):
                        ins = nc.tensor.matmul(U_BANK[:, C * t:C * (t + 1)], part[:, k, P * t:P * (t + 1)],
                                               wu[:], start=ends[0], stop=ends[1])
                ins.then_inc(u_done, 1)

            def similarity(b):
                k, i0 = b // BPB, N * (b % BPB)
                pe.wait_ge(kq_stacked[0], 2 * (k + 1))
                pe.wait_ge(kq_stacked[1], 2 * (k + 1))
                if b >= 2:
                    pe.wait_ge(probs_ready, 2 * (b - 1))
                for i in range(2):
                    ins = nc.tensor.matmul(S_BANK[b % 2][:, N * i:N * (i + 1)],
                                           kq_left[:, k % 2, i0 + P * i:i0 + P * (i + 1)],
                                           kq_right[:, k % 2, i0:i0 + N], start=True, stop=True)
                ins.then_inc(sim_done, 1)

            def transpose_probs(b):
                pe.wait_ge(probs_ready, 2 * (b + 1))
                if b >= 2:
                    pe.wait_ge(probsT_copied[b % 2], b // 2)
                for i in range(2):
                    for j in range(2):
                        ins = nc.tensor.transpose(PT_BANK[b % 2][:, N * j + P * i:N * j + P * (i + 1)],
                                                  probs[:, b % 2, i, P * j:P * (j + 1)], ident[:])
                ins.then_inc(probsT_done, 1)

            def attend(b):
                at = (b % BPB) * 2 * (C + 1)
                pe.wait_ge(probsT_copied[b % 2], b // 2 + 1)
                pe.wait_ge(u_copied, b // BPB + 1)
                if b >= 2:
                    pe.wait_ge(t_ready, TPB * (b // BPB))
                for i in range(2):
                    for j in range(2):
                        ins = nc.tensor.matmul(O_BANK[:, at + (C + 1) * i:at + (C + 1) * (i + 1)],
                                               probsT[:, b % 2, j, P * i:P * (i + 1)], u_sb[:, 2 * b + j, :],
                                               start=(j == 0), stop=(j == 1))
                ins.then_inc(attn_done, 1)

            def transpose_t(k):
                pe.wait_ge(tn_ready, k + 1)
                pe.wait_ge(x_lo_ready, NBLK)
                if k >= 1:
                    pe.wait_ge(lo_ready, k)
                for t in range(TPB):
                    ins = nc.tensor.transpose(T_BANK[:, P * t:P * (t + 1)], tn[:, k % 2, t, :, :], ident[:])
                ins.then_inc(tnT_done, 1)

            def route(k):
                pe.wait_ge(lo_ready, k + 1)
                pe.wait_ge(kq_lo_ready, NBLK)
                if k >= 1:
                    pe.wait_ge(logits_copied, k)
                for t in range(TPB):
                    own = slice(BLK * k + P * t, BLK * k + P * (t + 1))
                    for part, ends in ((t_hi, (True, False)), (t_lo, (False, True))):
                        ins = nc.tensor.matmul(K_BANK[:, E * t:E * (t + 1)], part[:, own], router[:],
                                               start=ends[0], stop=ends[1])
                ins.then_inc(logits_done, 1)

            pe.wait_ge(consts_loaded, 16 * CONST_DMAS)
            pe.wait_ge(consts_made, 3)
            pe.wait_ge(dve_consts, 2)
            nc.tensor.matmul(bank[0][:, 0:C], wv, wo, start=True, stop=True).then_inc(wu_done, 1)
            nc.tensor.matmul(bank[1][:, 0:C], bv.to_broadcast([CK, P]), wo, start=True, stop=False)
            nc.tensor.matmul(bank[1][:, 0:C], ones_row[:], bo[:], start=False, stop=True).then_inc(bias_done, 1)
            transpose_x(0)
            pe.wait_ge(dve_consts, 5)
            key_query(0)
            value_out(0)
            pe.wait_ge(bias_copied, 1)
            similarity(0)
            similarity(1)
            transpose_x(1)
            transpose_probs(0)
            transpose_probs(1)
            key_query(1)
            value_out(1)
            for k in range(NBLK):
                if k >= 1:
                    transpose_probs(BPB * k)
                    transpose_probs(BPB * k + 1)
                if k + 1 < NBLK:
                    similarity(BPB * (k + 1))
                    similarity(BPB * (k + 1) + 1)
                if k >= 2:
                    route(k - 2)
                attend(BPB * k)
                if k + 2 < NBLK:
                    transpose_x(k + 2)
                attend(BPB * k + 1)
                if k + 2 < NBLK:
                    key_query(k + 2)
                    value_out(k + 2)
                if k >= 1:
                    transpose_t(k - 1)

            def up(base, place, first):
                blk, s = divmod(place, STEPS)
                n = step_no(base, place)
                q, j = divmod(s, CHUNKS)
                if place < STEPS and j == 0:
                    pe.wait_ge(w_hi_made, 3 * (q + 1))
                    pe.wait_ge(w_lo_made, 3 * (q + 1))
                own = bass.ds((base + blk) * BLK, BLK)
                for split, banks, freed, done in ((w1_split, H1_BANK, silu_done, h1_done),
                                                  (w3_split, H3_BANK, hid_done, h3_done)):
                    w = split[:, q, P * j:P * (j + 1)]
                    if not (first and place < 2):
                        pe.wait_ge(freed, n - 1)
                    nc.tensor.matmul(banks[s % 2][:], w, t_hi[:, own], start=True, stop=False)
                    nc.tensor.matmul(banks[s % 2][:], w, t_lo[:, own], start=False, stop=True).then_inc(done, 1)

            def down(base, place, first):
                blk, s = divmod(place, STEPS)
                q, j = divmod(s, CHUNKS)
                pe.wait_ge(hid_hi_made, step_no(base, place) + 1)
                lo_wait(pe, base, place)
                slots = ([(0, j)] if j <= SEAM else []) + ([(1, j - SEAM)] if j >= SEAM else [])
                for side, slot in slots:
                    if slot == 0 and not (first and q == 0):
                        pe.wait_ge(y_gated, (base + blk) * E + 2 * q + side - 1)
                    w = w2_split[:, 2 * SLOTS * q + SLOTS * side + slot, :, :]
                    nc.tensor.matmul(Y_BANK[side][:], w, hid_hi[:, s % RING, :], start=(slot == 0), stop=False)
                    ins = nc.tensor.matmul(Y_BANK[side][:], w, hid_lo[:, s % RING, :], start=False,
                                           stop=(slot == SEAM))
                ins.then_inc(hid_used, 1)

            def tick(base, place, first, tail):
                blk, s = divmod(place, STEPS)
                if not tail:
                    up(base, place, first)
                if first and place == ROUTE_AT - 3:
                    route(NBLK - 2)
                if first and place == ROUTE_AT - 2:
                    transpose_t(NBLK - 1)
                if first and place == ROUTE_AT - 1:
                    route(NBLK - 1)
                if first and place == TURN_AT:
                    pe.wait_ge(gates_ready, 1)
                    nc.tensor.transpose(bank[6][:, 0:P], gates[:], ident[:]).then_inc(gates_turned, 1)
                if s == TRANSPOSE_T_AT and not tail:
                    pe.wait_ge(t_staged, base + blk + 1)
                    if not first:
                        pe.wait_ge(tT_copied, base + blk)
                    for t in range(TPB):
                        ins = nc.tensor.transpose(bank[7][:, P * t:P * (t + 1)], t_stage[:, t, :, :], ident[:])
                    ins.then_inc(tT_done, 1)
                if place >= LAG and (not tail or place - LAG < STEPS):
                    down(base, place - LAG, first)

            run_blocks(pe, tick)


def kernel(**inputs):
    import numpy as np
    import concourse.bacc as bacc
    from concourse.bass_utils import run_bass_kernel_spmd

    a = {k: np.asarray(v) for k, v in inputs.items()}

    def experts(w):
        w = w.reshape(PAIRS, 2 * H, C).transpose(2, 0, 1)
        return np.concatenate([w, np.zeros((C, PAIRS, PW - 2 * H), w.dtype)], axis=2)

    w2 = np.zeros((PAIRS, 2, SLOTS * P, C), a["L0_ffn_w2"].dtype)
    rows = a["L0_ffn_w2"].transpose(0, 2, 1).reshape(PAIRS, 2, H, C)
    w2[:, 0, 0:H] = rows[:, 0]
    at = H - SEAM * P
    w2[:, 1, at:at + H] = rows[:, 1]
    arrays = {
        "x_tok": a["x"].reshape(B, C, N // P, P).transpose(3, 0, 2, 1).reshape(P, TILES, C),
        "projections": np.concatenate([np.tile(a["L0_conv_w_kq"].T, (2, 1)), np.tile(a["L0_ffn_router_w"].T, (2, 1)),
                                       np.tile(a["L0_conv_b_kq"], P // CK)[:, None]], axis=1),
        "value_output": np.concatenate([a["L0_conv_w_v"], a["L0_conv_w_v"], a["L0_conv_w_o"].T,
                                        a["L0_conv_b_v"][:, None]], axis=1),
        "b_o": a["L0_conv_b_o"][None],
        "w1_t": experts(a["L0_ffn_w1"]),
        "w3_t": experts(a["L0_ffn_w3"]),
        "w2_t": w2.reshape(PAIRS, 2 * SLOTS, P, C).transpose(2, 0, 1, 3),
    }
    arrays = {k: np.ascontiguousarray(v) for k, v in arrays.items()}
    nc = bacc.Bacc("TRN2", target_bir_lowering=False, num_devices=1)
    args = [nc.dram_tensor(k, v.shape, F32, kind="ExternalInput").ap() for k, v in arrays.items()]
    out = nc.dram_tensor("out", (B, C, N), F32, kind="ExternalOutput").ap()
    gates_dram = nc.dram_tensor("gates_dram", (TILES * E, P), F32).ap()
    metaformer(nc, *args, gates_dram, out.rearrange("b c n -> c b n"))
    got = run_bass_kernel_spmd(nc, [arrays], core_ids=[0]).results[0]["out"]
    return got.reshape(B, C, 16, 16)
```
